# Optimizing a Trainium2 kernel written in Bass

```python
import numpy as np
import jax
import jax.numpy as jnp

def _softmax(x, axis=-1):
    return jax.nn.softmax(x, axis=axis)

def _gelu(x):
    return jax.nn.gelu(x, approximate=True)

def _silu(x):
    return jax.nn.silu(x)

def _sigmoid(x):
    return jax.nn.sigmoid(x)

def _layernorm(x, axis=-1, eps=1e-05):
    m = jnp.mean(x, axis=axis, keepdims=True)
    v = jnp.var(x, axis=axis, keepdims=True)
    return (x - m) / jnp.sqrt(v + eps)

def _scatter_add(tgt, idx, src, axis=0):
    return tgt.at[idx].add(src)

def _segment_sum(src, seg, n):
    return jax.ops.segment_sum(src, seg, n)
kernel_name = 'mk_macaron_d1_jaxref_r2_d80416'

def setup_inputs(seed: int=0):
    np.random.seed(seed)
    _w = jnp.asarray

    def _L0_attn_setup():
        import jax, jax.numpy as jnp
        import numpy as np
        BSZ, T, D, N, R = (2, 1024, 1024, 16, 128)
        key = jax.random.key(seed)
        ks = jax.random.split(key, 5)
        x = jax.random.normal(ks[0], (BSZ, T, D), dtype=jnp.float32)
        W_xproj = jax.random.normal(ks[1], (R + 2 * N, D), dtype=jnp.float32) * 0.02
        W_dt = jax.random.normal(ks[2], (D, R), dtype=jnp.float32) * 0.02
        b_dt = jnp.exp(jax.random.uniform(ks[3], (D,), minval=np.log(0.001), maxval=np.log(0.1)).astype(jnp.float32))
        A_log = jax.random.normal(ks[4], (D, N), dtype=jnp.float32) * 0.01
        D_param = jnp.ones((D,), dtype=jnp.float32)
        return {'x': x, 'W_xproj': W_xproj, 'W_dt': W_dt, 'b_dt': b_dt, 'A_log': A_log, 'D_param': D_param}
    _L0_attn_in = _L0_attn_setup()

    def _L0_ffn_setup():
        import jax, jax.numpy as jnp
        import numpy as np
        TOPK = 4
        key = jax.random.key(seed)
        k_x, k_a, k_b, k_w, k_bias = jax.random.split(key, 5)
        b, s, h, j, a, r = (4, 1024, 1024, 1024, 64, 16)
        x = jax.random.normal(k_x, (b, s, h), dtype=jnp.float32)
        A = jax.random.normal(k_a, (a, r, h), dtype=jnp.float32) * 0.02
        B = jax.random.normal(k_b, (a, j, r), dtype=jnp.float32) * 0.02
        W = jax.random.normal(k_w, (j, h), dtype=jnp.float32) * 0.02
        bias = jax.random.normal(k_bias, (j,), dtype=jnp.float32) * 0.02
        return {'x': x, 'A': A, 'B': B, 'W': W, 'bias': bias}
    _L0_ffn_in = _L0_ffn_setup()
    _d = {'L0_attn_x': _L0_attn_in['x'], 'L0_attn_W_xproj': _L0_attn_in['W_xproj'], 'L0_attn_W_dt': _L0_attn_in['W_dt'], 'L0_attn_b_dt': _L0_attn_in['b_dt'], 'L0_attn_A_log': _L0_attn_in['A_log'], 'L0_attn_D_param': _L0_attn_in['D_param'], 'L0_ffn_A': _L0_ffn_in['A'], 'L0_ffn_B': _L0_ffn_in['B'], 'L0_ffn_W': _L0_ffn_in['W'], 'L0_ffn_bias': _L0_ffn_in['bias']}
    _x0 = _d['L0_attn_x']
    _d['L0_attn_x'] = jax.random.normal(jax.random.fold_in(jax.random.key(seed), 1), (2, 2048, 1024), dtype=_x0.dtype)
    del _x0
    return _d

def reference(L0_attn_x, L0_attn_W_xproj, L0_attn_W_dt, L0_attn_b_dt, L0_attn_A_log, L0_attn_D_param, L0_ffn_A, L0_ffn_B, L0_ffn_W, L0_ffn_bias):

    def _L0_attn_ref(x, W_xproj, W_dt, b_dt, A_log, D_param):
        import jax, jax.numpy as jnp
        import numpy as np
        BSZ, T, D, N, R = (2, 1024, 1024, 16, 128)
        r = W_dt.shape[1]
        n = A_log.shape[1]
        xz = jnp.einsum('btd,rd->btr', x, W_xproj)
        delta_r = xz[..., :r]
        B_mat = xz[..., r:r + n]
        C_mat = xz[..., r + n:]
        delta = jax.nn.softplus(jnp.einsum('btr,dr->btd', delta_r, W_dt) + b_dt)
        A = -jnp.exp(A_log)
        dA = jnp.exp(delta[..., None] * A)
        Bu = delta[..., None] * B_mat[:, :, None, :] * x[..., None]

        def step(h, inp):
            dA_t, Bu_t, C_t = inp
            h = dA_t * h + Bu_t
            y = jnp.sum(h * C_t[:, None, :], axis=-1)
            return (h, y)
        h0 = jnp.zeros((x.shape[0], x.shape[2], n), dtype=Bu.dtype)
        _, ys = jax.lax.scan(step, h0, (dA.swapaxes(0, 1), Bu.swapaxes(0, 1), C_mat.swapaxes(0, 1)))
        y = ys.swapaxes(0, 1)
        return y + x * D_param

    def _L0_ffn_ref(x, A, B, W, bias):
        import jax, jax.numpy as jnp
        import numpy as np
        TOPK = 4
        vecs = jnp.einsum('arh,bsh->bsar', A, x)
        arrows = jnp.linalg.norm(vecs, axis=-1)
        _, idx = jax.lax.top_k(arrows, TOPK)
        routes = jax.nn.one_hot(idx, arrows.shape[-1], dtype=x.dtype).sum(-2) / TOPK
        v = jnp.einsum('bsa,bsar->bsr', routes, vecs)
        delta = jnp.einsum('bsa,ajr,bsr->bsj', routes, B, v)
        base = jnp.einsum('bsh,jh->bsj', x, W) + bias
        return base + delta
    x = L0_attn_x
    x = x + 0.5 * _L0_ffn_ref(_layernorm(x, axis=-1), L0_ffn_A, L0_ffn_B, L0_ffn_W, L0_ffn_bias)
    x = x + _L0_attn_ref(_layernorm(x, axis=-1), L0_attn_W_xproj, L0_attn_W_dt, L0_attn_b_dt, L0_attn_A_log, L0_attn_D_param)
    x = x + 0.5 * _L0_ffn_ref(_layernorm(x, axis=-1), L0_ffn_A, L0_ffn_B, L0_ffn_W, L0_ffn_bias)
    return x

_drawn_inputs = setup_inputs


def setup_inputs(seed=0):
    import zlib

    import numpy as np

    out = dict(_drawn_inputs(seed))
    spreads = {'L0_attn_D_param': (1.0, 0.2)}
    factors = {'L0_attn_b_dt': 5.578, 'L0_attn_A_log': 8.0, 'L0_ffn_A': 3.11, 'L0_ffn_bias': 3.66}
    for name, (base, spread) in spreads.items():
        noise = np.random.default_rng([zlib.crc32(name.encode()), seed]).standard_normal(out[name].shape)
        drawn = base * np.exp(spread * noise) if base else spread * noise
        out[name] = jnp.asarray(drawn.astype(out[name].dtype))
    for name, factor in factors.items():
        out[name] = (out[name] * factor).astype(out[name].dtype)
    return out
```

```python
import concourse.bass as bass
from concourse import mybir
from contextlib import ExitStack

P = 128
TC = 256
NH = 8
TOPK = 4
EPS = 1e-5
X_SCALE = 1024.0
V_SCALE = 2.0 ** -21
POOL_C = 5


def build(nc, x, AT, BT, WT, bias, WxT, WdtT, b_dt, A_log, D_par, out):
    f32, f16, bf16, i32 = mybir.dt.float32, mybir.dt.float16, mybir.dt.bfloat16, mybir.dt.int32
    ALU, ACT, AX = mybir.AluOpType, mybir.ActivationFunctionType, mybir.AxisListType
    RMAX = bass.bass_isa.ReduceOp.max

    BSZ, T, D = x.shape
    KD = D // P
    R16 = 16
    NE = AT.shape[1] // R16
    NS = A_log.shape[2]
    RX = WdtT.shape[0]
    NX = WxT.shape[1]
    NTOK = BSZ * T
    UB = T // P
    GB = UB // 2
    NF1 = BSZ * UB
    HF = D // 2
    KB = KD // 2
    NT = 2 * KD
    SLOT_TILES = [len(range(n, KD, 3)) for n in range(3)]

    x_r = x.rearrange("b t d -> (b t) d")
    out_r = out.rearrange("b t d -> (b t) d")
    x2_d = nc.dram_tensor("x2_scratch", (NTOK, D), f32, kind="Internal").ap()
    xnT_d = nc.dram_tensor("xnT_scratch", (NTOK, D), f32, kind="Internal").ap()
    yT_d = nc.dram_tensor("yT_scratch", (NTOK, D), f32, kind="Internal").ap()
    dr_d = nc.dram_tensor("delta_rank_scratch", (NTOK, P), f32, kind="Internal").ap()
    bc_d = nc.dram_tensor("bc_scratch", (NTOK, P), f32, kind="Internal").ap()
    xnT_u = xnT_d.rearrange("(u p) (k t) -> p u k t", p=P, t=P)
    yT_u = yT_d.rearrange("(u p) (k t) -> p u k t", p=P, t=P)
    dr_u = dr_d.rearrange("(u p) t -> p u t", p=P)
    bc_u = bc_d.rearrange("(u n) t -> n u t", n=P)

    ctx = ExitStack()
    with ctx:
        def sb(name, shape, dt=f32):
            return ctx.enter_context(nc.sbuf_tensor(name, shape, dt))

        def sem(name):
            return ctx.enter_context(nc.semaphore(name))

        wA = sb("wA", [P, 2, KD, D], f16)
        wB = sb("wB", [P, 2, KD, D], f16)
        wW = sb("wW", [P, 2, KD, D], f16)
        wx = sb("wx", [P, KD, NX])
        wdt = sb("wdt", [RX, D])
        mreg = sb("mreg", [P, 2 * NS * TC + 3 * (NH + 1) * TC + 9 * TC])
        o = 0
        Bb = mreg[:, o:o + NS * TC].rearrange("p (n t) -> p n t", n=NS); o += NS * TC
        Cb = mreg[:, o:o + NS * TC].rearrange("p (n t) -> p n t", n=NS); o += NS * TC
        Tr = mreg[:, o:o + 3 * (NH + 1) * TC].rearrange("p (s n t) -> p s n t", s=3, n=NH + 1); o += 3 * (NH + 1) * TC
        xt = mreg[:, o:o + 3 * TC].rearrange("p (s t) -> p s t", s=3); o += 3 * TC
        dl = mreg[:, o:o + 2 * TC].rearrange("p (s t) -> p s t", s=2); o += 2 * TC
        dx = mreg[:, o:o + 2 * TC].rearrange("p (s t) -> p s t", s=2); o += 2 * TC
        lab = mreg[:, o:o + TC]; o += TC
        drT = mreg[:, o:o + TC]; o += TC
        stage = [mreg[:, n * KD * D:(n + 1) * KD * D].rearrange("p (k n) -> p k n", k=KD) for n in range(2)]
        xin = sb("xin", [P, 2, D])
        xn = sb("xn", [P, D])
        aux = sb("aux", [P, KD, P])
        auxf = aux[:, :, :].rearrange("p k t -> p (k t)")
        xT = sb("xT", [P, 2, KD, P], f16)
        sel = sb("sel", [P, D])
        sel3 = sel[:, :].rearrange("p (a r) -> p a r", r=R16)
        un = sel[:, :].bitcast(f16).rearrange("p (c a r) -> p c a r", c=2, r=R16)
        un2 = sel[:, :].bitcast(f16).rearrange("p (c k q) -> p c k q", c=2, k=KD)
        uT = sb("uT", [P, 2, KD, P], f16)
        drs = sb("drs", [P, P])
        bcs = sb("bcs", [P, P])
        brow = sb("brow", [P, D], bf16)
        onesb = sb("onesb", [P, P], bf16)
        idf = sb("idf", [P, P])
        idh = sb("idh", [P, P], f16)
        nA = sb("nA", [P, KD, NS])
        hst = sb("hst", [P, KD, NS])
        bdt = sb("bdt", [P, KD])
        Dp = sb("Dp", [P, KD])
        n2 = sb("n2", [P, NE + 4])
        n2m = sb("n2m", [P, NE + 4])
        top = sb("top", [P, 8])
        mask = sb("mask", [P, NE])
        vs = sb("vs", [P, R16])
        vh = sb("vh", [P, 2, R16], f16)
        amx = sb("amx", [P, 4])
        amr = sb("amr", [P, 4])
        sc = sb("sc", [P, 16])
        lnb = {n: {k: sb(f"{n}_{k}", [P, w]) for k, w in
                   (("st", 12), ("mv", 2), ("ve", 1), ("r0", 1), ("t", 1), ("r", 1), ("nm", 1))} for n in ("ln1", "ln2")}

        def pb(name, shape, dt=f32):
            return ctx.enter_context(nc.psum_tensor(name, shape, dt))

        pv = pb("pv", [P, 2, HF])
        po = pb("po", [P, 2, HF])
        pt = pb("pt", [P, HF])
        pA = pb("pA", [P, 2, 2, TC])
        pz = pb("pz", [P, HF])
        pth = pt[:, :].bitcast(f16)

        s_wld = [sem(f"s_wld{n}") for n in range(3)]
        s_cst = sem("s_cst"); s_idz = sem("s_idz"); s_id = sem("s_id"); s_amx = sem("s_amx"); s_amr = sem("s_amr")
        s_scl = sem("s_scl"); s_whi = sem("s_whi"); s_wlo = sem("s_wlo"); s_bp = sem("s_bp"); s_bmv = sem("s_bmv")
        s_nA = sem("s_nA")
        s_set = sem("s_set")
        s_ldx = [sem(f"s_ldx{n}") for n in range(2)]
        s_ldy = sem("s_ldy")
        s_stx = [sem(f"s_stx{n}") for n in range(2)]
        s_stn = sem("s_stn"); s_stp = sem("s_stp")
        s_mv = sem("s_mv"); s_sd = sem("s_sd"); s_rs = sem("s_rs"); s_xn = sem("s_xn")
        s_xT = sem("s_xT"); s_xhi = sem("s_xhi"); s_xlo = sem("s_xlo")
        s_vec = sem("s_vec"); s_sq = sem("s_sq"); s_gm = sem("s_gm"); s_u = sem("s_u"); s_uT = sem("s_uT"); s_uc = sem("s_uc")
        s_base = sem("s_base")
        s_out = sem("s_out"); s_res = sem("s_res")
        s_mv2 = sem("s_mv2"); s_sd2 = sem("s_sd2"); s_rs2 = sem("s_rs2"); s_xn2 = sem("s_xn2")
        s_nT = sem("s_nT"); s_nc = sem("s_nc"); s_pj = sem("s_pj"); s_pc = sem("s_pc")
        s_yT = sem("s_yT"); s_ya = sem("s_ya")
        s_ldr = sem("s_ldr"); s_ldb = [sem(f"s_ldb{n}") for n in range(2)]; s_ldc = [sem(f"s_ldc{n}") for n in range(2)]
        s_ldt = [sem(f"s_ldt{n}") for n in range(3)]; s_sty = [sem(f"s_sty{n}") for n in range(3)]
        s_z = sem("s_z"); s_ab = sem("s_ab"); s_l = sem("s_l"); s_zm = sem("s_zm"); s_dl = sem("s_dl"); s_dx = sem("s_dx")
        s_dA = sem("s_dA"); s_dAf = [sem(f"s_dAf{n}") for n in range(2)]
        s_bu = sem("s_bu"); s_h = sem("s_h"); s_cm = sem("s_cm"); s_rd = sem("s_rd"); s_y = sem("s_y")

        block = ctx.enter_context(nc.Block())

        def num(g, p):
            return g * 2 + p

        def after(g, p):
            return (g, 1) if p == 0 else (g + 1, 0)

        def phases(eng, pair, opening, between):
            def run(first, end, chunk, kind, peel_first, peel_last):
                if peel_first:
                    pair(first, chunk(first), kind, False)
                with eng.Fori(first + peel_first, end - peel_last) as g:
                    pair(g, chunk(g), kind, False)
                if peel_last:
                    pair(end - 1, chunk(end - 1), kind, True)

            opening(0, 1)
            run(0, GB, lambda g: None, 1, 1, 0)
            between(1)
            run(GB, 2 * GB, lambda g: g - GB, 1, 1, 1)
            between(2)
            opening(2 * GB, 2)
            run(2 * GB, 3 * GB, lambda g: g - GB, 2, 1, 1)
            between(3)
            opening(3 * GB, 2)
            run(3 * GB, 4 * GB, lambda g: None, 2, 0, 1)

        @block.sync
        def _(sp):
            sp.dma_start(stage[0], AT.rearrange("(k p) n -> p k n", p=P)).then_inc(s_wld[0], 16)
            sp.dma_start(stage[1], WT.rearrange("(k p) n -> p k n", p=P)).then_inc(s_wld[2], 16)
            sp.dma_start(bdt[:, :], b_dt).then_inc(s_cst, 16)
            sp.dma_start(Dp[:, :], D_par).then_inc(s_cst, 16)
            sp.dma_start(nA[:, :, :], A_log).then_inc(s_cst, 16)
            sp.dma_start(wx[:, :, :], WxT.rearrange("(k p) n -> p k n", p=P)).then_inc(s_cst, 16)
            sp.dma_start(wdt[:, :], WdtT).then_inc(s_cst, 16)
            sp.dma_start(uT[0:1, :, :, :].rearrange("p c k t -> p (c k t)").bitcast(f32), bias).then_inc(s_cst, 16)
            sp.wait_ge(s_whi, 1)
            sp.wait_ge(s_wlo, 1)
            sp.dma_start(stage[0], BT.rearrange("(k p) n -> p k n", p=P)).then_inc(s_wld[1], 16)
            sp.wait_ge(s_bp, 1)
            for n in range(2):
                sp.dma_start(brow[n + 1:n + 2, :], auxf[0:1, n * HF:(n + 1) * HF].bitcast(bf16)).then_inc(s_bmv, 16)

            def pieces(a):
                return a.rearrange("p (u t) -> p u t", t=P)

            def load_unit(g, p, kind):
                u = num(g, p)
                row = (u if kind == 1 else u - NF1) * P
                sp.wait_ge(s_stx[p], g * 16)
                if kind == 1:
                    sp.dma_start(xin[:, p, :], x_r[bass.ds(row, P), :]).then_inc(s_ldx[p], 16)
                else:
                    sp.dma_start(xin[:, p, :], x2_d[bass.ds(row, P), :]).then_inc(s_ldx[p], 16)
                    sp.wait_ge(s_yT, (u - NF1) * 2)
                    sp.dma_start(aux[:, :, :], yT_d[bass.ds(row, P), :].rearrange("p (k t) -> p k t", t=P)).then_inc(s_ldy, 16)

            def load_tile(q, dt, first):
                sp.wait_ge(s_sty[dt % 3], q * (16 * SLOT_TILES[dt % 3]) + 16 * (dt // 3))
                sp.dma_start(pieces(xt[:, dt % 3, :]), xnT_u[:, bass.ds(first, 2), dt, :]).then_inc(s_ldt[dt % 3], 16)

            def store_tile(q, dt, first):
                sp.wait_ge(s_y, q * KD + dt + 1)
                sp.dma_start(yT_u[:, bass.ds(first, 2), dt, :], pieces(xt[:, dt % 3, :])).then_inc(s_sty[dt % 3], 16)

            def spread(q, h, what, first):
                dst, row = (Bb, 0) if what == "b" else (Cb, NS)
                s = (s_ldb if what == "b" else s_ldc)[h]
                for n in range(2):
                    src = bc_u[row + h * NH:row + (h + 1) * NH, bass.ds(first + n, 1), :].rearrange("n u t -> n (u t)")
                    sp.dma_start(dst[:, h * NH:(h + 1) * NH, n * P:(n + 1) * P], src.partition_broadcast(P)).then_inc(s, 16)

            def load_chunk(q):
                first = q * 2
                sp.wait_ge(s_z, q * KD)
                sp.dma_start(pieces(drT), dr_u[:, bass.ds(first, 2), :]).then_inc(s_ldr, 16)
                for h in range(2):
                    sp.wait_ge(s_bu, q * NT)
                    spread(q, h, "b", first)
                for dt in range(3):
                    load_tile(q, dt, first)
                for h in range(2):
                    sp.wait_ge(s_rd, q * NT)
                    spread(q, h, "c", first)

            def opening(g, kind):
                load_unit(g, 0, kind)

            def between(phase):
                if phase == 1:
                    sp.wait_ge(s_stn, 16 * UB)
                    sp.wait_ge(s_stp, 32 * UB)
                if phase == 2:
                    sp.wait_ge(s_stn, 16 * NF1)
                    sp.wait_ge(s_stp, 32 * NF1)
                if phase > 1:
                    for n in range(2):
                        sp.wait_ge(s_stx[n], 16 * (phase * GB))
                    for n in range(3):
                        sp.wait_ge(s_sty[n], 16 * (phase - 1) * GB * SLOT_TILES[n])
                if phase in (1, 2):
                    load_chunk((phase - 1) * GB)

            def pair(g, q, kind, last):
                first = None if q is None else q * 2
                for p in range(2):
                    u = num(g, p)
                    row = (u if kind == 1 else u - NF1) * P
                    g2, p2 = after(g, p)
                    if not (last and p == 1):
                        load_unit(g2, p2, kind)
                    for i in range(KD // 2):
                        if i == 2:
                            sp.wait_ge(s_res, u * 2 + 2)
                            dst = (x2_d if kind == 1 else out_r)[bass.ds(row, P), :]
                            sp.dma_start(dst, xin[:, p, :]).then_inc(s_stx[p], 16)
                        if q is not None:
                            dt = p * (KD // 2) + i - 1
                            if dt >= 0:
                                store_tile(q, dt, first)
                                if dt + 3 < KD:
                                    load_tile(q, dt + 3, first)
                    if kind == 1:
                        sp.wait_ge(s_nc, u * 2 + 2)
                        sp.dma_start(xnT_d[bass.ds(row, P), :], auxf).then_inc(s_stn, 16)
                        sp.wait_ge(s_pc, u + 1)
                        sp.dma_start(dr_d[bass.ds(row, P), :], drs[:, :]).then_inc(s_stp, 16)
                        sp.dma_start(bc_d[bass.ds(row, 2 * NS), :], bcs[P - 2 * NS:P, :]).then_inc(s_stp, 16)
                if q is not None:
                    store_tile(q, KD - 1, first)
                if q is not None and not last:
                    load_chunk(q + 1)

            phases(sp, pair, opening, between)
            for n in range(2):
                sp.wait_ge(s_stx[n], 16 * 4 * GB)

        @block.gpsimd
        def _(pool):
            pool.memset(idf[:, :], 0.0).then_inc(s_idz, 1)
            pool.memset(idh[:, :], 0.0).then_inc(s_idz, 1)
            pool.wait_ge(s_idz, 2)
            for m in (idf, idh):
                pool.affine_select(out=m[:, :], in_=m[:, :], compare_op=ALU.not_equal, fill=1.0, base=0,
                                   pattern=[[-1, P]], channel_multiplier=1).then_inc(s_id, 1)
            pool.memset(onesb[:, :], 1.0).then_inc(s_id, 1)
            for n in range(3):
                pool.wait_ge(s_amx, n + 1)
                pool.partition_all_reduce(amr[:, n:n + 1], amx[:, n:n + 1], P, RMAX).then_inc(s_amr, 1)

            def times_b(q, k):
                dt, h = k // 2, k % 2
                if k % 2 == 0:
                    pool.wait_ge(s_dx, q * KD + dt + 1)
                if dt == 0:
                    pool.wait_ge(s_ldb[h], q * 32 + 32)
                pool.wait_ge(s_rd, q * NT + max(k - 2, 0))
                dst = Tr[:, k % 3, 0:NH, :]
                pool.tensor_tensor(dst, Bb[:, h * NH:(h + 1) * NH, :],
                                   dx[:, dt % 2, :].unsqueeze(1).broadcast_to([P, NH, TC]), ALU.mult).then_inc(s_bu, 1)

            def times_c(q, k):
                dt, h = k // 2, k % 2
                pool.wait_ge(s_h, q * NT + k + 1)
                if dt == 0:
                    pool.wait_ge(s_ldc[h], q * 32 + 32)
                dst = Tr[:, k % 3, 0:POOL_C, :]
                pool.tensor_tensor(dst, dst, Cb[:, h * NH:h * NH + POOL_C, :], ALU.mult).then_inc(s_cm, 1)

            def chunk(q):
                times_b(q, 0)
                for k in range(NT):
                    if k + 1 < NT:
                        times_b(q, k + 1)
                    times_c(q, k)

            chunk(0)
            with pool.Fori(1, BSZ * GB) as q:
                chunk(q)

        @block.tensor
        def _(pe):
            pe.wait_ge(s_id, 3)

            def blocks(dst, src, sem_done, idt):
                for k in range(KB):
                    last = nc.tensor.transpose(dst[:, k * P:(k + 1) * P], src(k), idt)
                last.then_inc(sem_done, 1)

            def norm_blocks(g, p, half):
                u = num(g, p)
                if half == 0:
                    pe.wait_ge(s_xn, u + 1)
                else:
                    pe.wait_ge(s_xhi, u * 2 + 1)
                    pe.wait_ge(s_xlo, u * 2 + 1)
                blocks(pt, lambda k: xn[:, (half * KB + k) * P:(half * KB + k + 1) * P], s_xT, idf[:, :])

            def y_blocks(g, p, half):
                v = num(g, p) - NF1
                if half == 0:
                    pe.wait_ge(s_ldy, v * 16 + 16)
                else:
                    pe.wait_ge(s_ya, v * 2 + 1)
                blocks(pt, lambda k: aux[:, half * KB + k, :], s_yT, idf[:, :])

            def product(dst, lhs, w, nb, first, stop):
                for k in range(KD):
                    for n, (a, b) in enumerate(((0, 0), (0, 1), (1, 0))):
                        last = nc.tensor.matmul(dst, lhs[:, a, k, :], w[:, b, k, nb * HF:(nb + 1) * HF],
                                                start=(first and k == 0 and n == 0), stop=(stop and k == KD - 1 and n == 2))
                return last

            def experts(g, p, nb):
                u = num(g, p)
                if nb == 0:
                    pe.wait_ge(s_xhi, u * 2 + 2)
                    pe.wait_ge(s_xlo, u * 2 + 2)
                    pe.wait_ge(s_gm, u)
                product(pv[:, nb, :], xT, wA, nb, True, True).then_inc(s_vec, 1)

            def base(g, p, nb):
                u = num(g, p)
                pe.wait_ge(s_res, u * 2)
                nc.tensor.matmul(po[:, nb, :], onesb[:, :], brow[:, nb * HF:(nb + 1) * HF], start=True, stop=False)
                product(po[:, nb, :], xT, wW, nb, False, False)

            def routed_blocks(g, p, part):
                u = num(g, p)
                pe.wait_ge(s_u, u * 2 + 1 + part)
                if part == 1:
                    pe.wait_ge(s_uc, u * 2 + 1)
                for k in range(KD):
                    last = nc.tensor.transpose(pth[:, k * P:(k + 1) * P], un2[:, part, k, :], idh[:, :])
                last.then_inc(s_uT, 1)

            def routed(g, p, nb):
                u = num(g, p)
                if nb == 0:
                    pe.wait_ge(s_uc, u * 2 + 2)
                product(po[:, nb, :], uT, wB, nb, False, True).then_inc(s_out, 1)

            def scan_inputs(g, p):
                u = num(g, p)
                pe.wait_ge(s_xn2, u + 1)
                for half in range(2):
                    if half:
                        pe.wait_ge(s_nc, u * 2 + 1)
                    blocks(pt, lambda k: xn[:, (half * KB + k) * P:(half * KB + k + 1) * P], s_nT, idf[:, :])
                pe.wait_ge(s_nc, u * 2 + 2)
                for n, col in enumerate((0, NX - P)):
                    for k in range(KD):
                        last = nc.tensor.matmul(pt[:, n * P:(n + 1) * P], wx[:, k, col:col + P], aux[:, k, :],
                                                start=(k == 0), stop=(k == KD - 1))
                last.then_inc(s_pj, 1)

            def z(q, dt):
                if dt == 0:
                    pe.wait_ge(s_ldr, q * 16 + 16)
                pe.wait_ge(s_ab, q * KD + dt)
                pe.wait_ge(s_zm, q * KD + dt)
                nc.tensor.matmul(pz[:, 0:TC], wdt[:, dt * P:(dt + 1) * P], drT[:, :], start=True, stop=True).then_inc(s_z, 1)

            def lead(g, p):
                norm_blocks(g, p, 0)
                norm_blocks(g, p, 1)

            def opening(g, kind):
                if kind == 2:
                    y_blocks(g, 0, 0)
                    y_blocks(g, 0, 1)
                    pe.wait_ge(s_ya, (num(g, 0) - NF1) * 2 + 2)
                lead(g, 0)
                for nb in range(2):
                    experts(g, 0, nb)

            def between(phase):
                pass

            pe.wait_ge(s_cst, 16 * 6)
            first = [True]

            def pair(g, q, kind, last):
                for p in range(2):
                    u = num(g, p)
                    g2, p2 = after(g, p)
                    more = not (last and p == 1)
                    d0 = p * (KD // 2)
                    if q is not None and p == 0:
                        z(q, 0)
                    base(g, p, 0)
                    if kind == 2 and more:
                        y_blocks(g2, p2, 0)
                    if q is not None:
                        z(q, d0 + 1)
                    base(g, p, 1)
                    if kind == 2 and more:
                        y_blocks(g2, p2, 1)
                        pe.wait_ge(s_ya, (u + 1 - NF1) * 2 + 2)
                    elif kind == 1:
                        pe.wait_ge(s_pc, u)
                    routed_blocks(g, p, 0)
                    routed_blocks(g, p, 1)
                    routed(g, p, 0)
                    if more:
                        norm_blocks(g2, p2, 0)
                    if q is not None:
                        z(q, d0 + 2)
                    routed(g, p, 1)
                    if more:
                        norm_blocks(g2, p2, 1)
                    if q is not None:
                        z(q, d0 + 3)
                    if more:
                        experts(g2, p2, 0)
                        experts(g2, p2, 1)
                    if q is not None and p == 0:
                        z(q, KD // 2)
                    if kind == 1:
                        scan_inputs(g, p)

            pe.wait_ge(s_wlo, 3)
            pe.wait_ge(s_whi, 3)
            pe.wait_ge(s_bmv, 32)
            phases(pe, pair, opening, between)

        @block.scalar
        def _(act):
            act.preload_act_table_set("natural_log_exp_and_others")
            for n, (w, st, col) in enumerate(((wA, 0, 0), (wB, 0, 1), (wW, 1, 2))):
                act.wait_ge(s_scl, 1 if n == 0 else 2)
                for k in range(KD):
                    last = nc.scalar.activation(w[:, 0, k, :], stage[st][:, k, :], ACT.Identity, scale=sc[:, col:col + 1])
                last.then_inc(s_whi, 1)
            act.wait_ge(s_cst, 16 * 6)
            nc.scalar.activation(nA[:, :, :], nA[:, :, :], ACT.Exp).then_inc(s_nA, 1)

            def seed(ln, s_in, s_done, u):
                b = lnb[ln]
                act.wait_ge(s_in, u + 1)
                nc.scalar.activation(b["r0"][:, :], b["ve"][:, :], ACT.Ln)
                act.drain()
                nc.scalar.activation(b["r0"][:, :], b["r0"][:, :], ACT.Exp, scale=-0.5).then_inc(s_done, 1)

            def normed(g, p):
                u = num(g, p)
                act.wait_ge(s_rs, u + 1)
                nc.scalar.activation(xn[:, :], xin[:, p, :], ACT.Identity, scale=lnb["ln1"]["r"][:, :],
                                     bias=lnb["ln1"]["nm"][:, :]).then_inc(s_xn, 1)

            def high(g, p, half):
                u = num(g, p)
                act.wait_ge(s_xT, u * 2 + 1 + half)
                nc.scalar.activation(xT[:, 0, half * KB:(half + 1) * KB, :].rearrange("p k t -> p (k t)"), pt[:, :],
                                     ACT.Copy).then_inc(s_xhi, 1)

            def squares(g, p, nb):
                u = num(g, p)
                act.wait_ge(s_vec, u * 2 + 1 + nb)
                if nb == 0:
                    act.wait_ge(s_uT, u * 2)
                nc.scalar.activation(sel[:, nb * HF:(nb + 1) * HF], pv[:, nb, :], ACT.Square).then_inc(s_sq, 1)

            def routed_copy(g, p, part):
                u = num(g, p)
                act.wait_ge(s_uT, u * 2 + 1 + part)
                nc.scalar.activation(uT[:, part, :, :].rearrange("p k t -> p (k t)"), pth[:, :], ACT.Copy).then_inc(s_uc, 1)

            def normed2(g, p):
                u = num(g, p)
                act.wait_ge(s_rs2, u + 1)
                act.wait_ge(s_xn2, u)
                nc.scalar.activation(xn[:, :], xin[:, p, :], ACT.Identity, scale=lnb["ln2"]["r"][:, :],
                                     bias=lnb["ln2"]["nm"][:, :]).then_inc(s_xn2, 1)

            def scan_input_copies(g, p, half):
                u = num(g, p)
                act.wait_ge(s_nT, u * 2 + 1 + half)
                if half == 0:
                    act.wait_ge(s_stn, u * 16)
                nc.scalar.activation(auxf[:, half * HF:(half + 1) * HF], pt[:, :], ACT.Copy).then_inc(s_nc, 1)

            def projection_copies(g, p):
                u = num(g, p)
                act.wait_ge(s_pj, u + 1)
                act.wait_ge(s_stp, u * 32)
                nc.scalar.activation(drs[:, :], pt[:, 0:P], ACT.Copy)
                nc.scalar.activation(bcs[P - 2 * NS:P, :], pt[P - 2 * NS:P, P:2 * P], ACT.Copy)
                act.drain().then_inc(s_pc, 1)

            def softplus(q, dt):
                m = q * KD + dt
                act.wait_ge(s_z, m + 1)
                act.wait_ge(s_dl, m)
                nc.scalar.activation(lab, pz[:, 0:TC], ACT.Abs, bias=bdt[:, dt:dt + 1]).then_inc(s_ab, 1)
                act.drain()
                nc.scalar.activation(lab, lab, ACT.Exp, scale=-1.0)
                act.drain()
                nc.scalar.activation(lab, lab, ACT.Ln, bias=1.0).then_inc(s_l, 1)

            def decays(q, k):
                dt, h = k // 2, k % 2
                if h == 0:
                    act.wait_ge(s_dl, q * KD + dt + 1)
                for j in range(NH // 2):
                    act.wait_ge(s_dAf[j % 2], q * (2 * NT) + 2 * k + j // 2)
                    for i in range(2):
                        n = h * NH + 2 * j + i
                        last = nc.scalar.activation(pA[:, j % 2, i, :], dl[:, dt % 2, :], ACT.Exp, scale=nA[:, dt, n:n + 1])
                    last.then_inc(s_dA, 1)

            def opening(g, kind):
                seed("ln1", s_mv, s_sd, num(g, 0))
                normed(g, 0)
                high(g, 0, 0)
                high(g, 0, 1)
                squares(g, 0, 0)
                squares(g, 0, 1)

            def between(phase):
                if phase == 1:
                    act.wait_ge(s_set, 1)

            def pair(g, q, kind, last):
                for p in range(2):
                    u = num(g, p)
                    g2, p2 = after(g, p)
                    more = not (last and p == 1)

                    def half(h):
                        if q is None:
                            return
                        k = p * KD + h
                        decays(q, k)
                        if h % 2 == 0 and k // 2 + 1 < KD:
                            softplus(q, k // 2 + 1)

                    if q is not None and p == 0:
                        softplus(q, 0)
                    half(0)
                    routed_copy(g, p, 0)
                    routed_copy(g, p, 1)
                    if more:
                        seed("ln1", s_mv, s_sd, u + 1)
                    half(1)
                    if more:
                        normed(g2, p2)
                    half(2)
                    if more:
                        high(g2, p2, 0)
                    half(3)
                    if more:
                        high(g2, p2, 1)
                    half(4)
                    if kind == 1:
                        seed("ln2", s_mv2, s_sd2, u)
                    half(5)
                    if kind == 1:
                        if more:
                            act.wait_ge(s_xT, u * 2 + 4)
                        normed2(g, p)
                    half(6)
                    if more:
                        squares(g2, p2, 0)
                        squares(g2, p2, 1)
                    if kind == 1:
                        scan_input_copies(g, p, 0)
                        scan_input_copies(g, p, 1)
                    half(7)
                    if kind == 1:
                        projection_copies(g, p)

            phases(act, pair, opening, between)

        @block.vector
        def _(dve):
            V = nc.vector
            V.memset(sc[:, :], 0.0)
            V.memset(brow[:, :], 0.0)
            V.memset(n2[:, NE:NE + 4], -1.0)
            order = ((0, 0, 0), (1, 0, 1), (2, 1, 2))
            dve.drain()

            def largest(n, st, ld):
                dve.wait_ge(s_wld[ld], 16)
                V.tensor_reduce(amx[:, n:n + 1], stage[st].rearrange("p k n -> p (k n)"), AX.X, ALU.max,
                                apply_absolute_value=True).then_inc(s_amx, 1)

            def power(n):
                dve.wait_ge(s_amr, n + 1)
                V.tensor_scalar(sc[:, 8:9].bitcast(i32), amr[:, n:n + 1].bitcast(i32), 0x7F800000, None, ALU.bitwise_and)
                dve.drain()
                V.tensor_scalar(sc[:, 8:9], sc[:, 8:9], 2.0 ** -40, 2.0 ** 40, ALU.max, ALU.min)
                dve.drain()
                V.reciprocal(sc[:, 9:10], sc[:, 8:9])
                dve.drain()
                V.tensor_scalar(sc[:, 4 + n:5 + n], sc[:, 9:10], 2.0 ** 13, None, ALU.mult)
                dve.drain()

            def low(w, st, col, n):
                dve.wait_ge(s_whi, n + 1)
                for k in range(KD):
                    last = V.scalar_tensor_tensor(w[:, 1, k, :], stage[st][:, k, :], sc[:, col:col + 1], w[:, 0, k, :],
                                                  ALU.mult, ALU.subtract)
                last.then_inc(s_wlo, 1)

            largest(*order[0])
            power(0)
            V.tensor_copy(sc[:, 0:1], sc[:, 4:5]).then_inc(s_scl, 1)
            low(wA, 0, 0, 0)
            largest(*order[1])
            largest(*order[2])
            power(1)
            power(2)
            V.tensor_tensor(sc[:, 10:11], sc[:, 4:5], sc[:, 5:6], ALU.mult)
            dve.drain()
            V.tensor_scalar(sc[:, 10:11], sc[:, 10:11], 2.0 ** -7, None, ALU.mult)
            V.tensor_scalar(sc[:, 11:12], sc[:, 6:7], X_SCALE, None, ALU.mult)
            dve.drain()
            V.tensor_tensor(sc[:, 12:13], sc[:, 10:11], sc[:, 11:12], ALU.min)
            V.reciprocal(sc[:, 13:14], sc[:, 4:5])
            dve.drain()
            V.tensor_scalar(sc[:, 1:2], sc[:, 12:13], sc[:, 13:14], 2.0 ** 7, ALU.mult, ALU.mult)
            V.reciprocal(sc[:, 14:15], sc[:, 12:13])
            V.tensor_scalar(sc[:, 2:3], sc[:, 12:13], 1.0 / X_SCALE, None, ALU.mult).then_inc(s_scl, 1)
            dve.drain()
            V.tensor_scalar(sc[:, 3:4], sc[:, 14:15], 0.5, None, ALU.mult)
            dve.wait_ge(s_cst, 16 * 6)
            brw = uT[0:1, :, :, :].rearrange("p c k t -> p (c k t)").bitcast(f32)
            b2, b3 = (auxf[0:1, n * HF:(n + 1) * HF].bitcast(bf16) for n in range(2))
            V.tensor_scalar(xn[0:1, :], brw, sc[0:1, 12:13], None, ALU.mult)
            dve.drain()
            V.tensor_copy(brow[0:1, :], xn[0:1, :])
            dve.drain()
            V.tensor_tensor(xn[0:1, :], xn[0:1, :], brow[0:1, :], ALU.subtract)
            dve.drain()
            V.tensor_copy(b2, xn[0:1, :])
            dve.drain()
            V.tensor_tensor(xn[0:1, :], xn[0:1, :], b2, ALU.subtract)
            dve.drain()
            V.tensor_copy(b3, xn[0:1, :]).then_inc(s_bp, 1)
            low(wB, 0, 1, 1)
            low(wW, 1, 2, 2)
            dve.wait_ge(s_nA, 1)
            V.tensor_scalar(nA[:, :, :], nA[:, :, :], -1.0, None, ALU.mult).then_inc(s_set, 1)

            def stats(ln, src, s_done):
                b = lnb[ln]
                for n in range(2):
                    V.bn_stats(b["st"][:, 6 * n:6 * n + 6], src[:, n * HF:(n + 1) * HF])
                dve.drain()
                V.bn_aggr(b["mv"][:, :], b["st"][:, :])
                dve.drain()
                V.tensor_scalar(b["ve"][:, :], b["mv"][:, 1:2], EPS, None, ALU.add).then_inc(s_done, 1)

            def refine(ln, scale, s_in, s_done, u):
                b = lnb[ln]
                dve.wait_ge(s_in, u + 1)
                V.scalar_tensor_tensor(b["t"][:, :], b["r0"][:, :], b["ve"][:, :], b["r0"][:, :], ALU.mult, ALU.mult)
                dve.drain()
                V.tensor_scalar(b["t"][:, :], b["t"][:, :], -0.5 * scale, 1.5 * scale, ALU.mult, ALU.add)
                dve.drain()
                V.tensor_tensor(b["r"][:, :], b["r0"][:, :], b["t"][:, :], ALU.mult)
                dve.drain()
                V.scalar_tensor_tensor(b["nm"][:, :], b["mv"][:, 0:1], -1.0, b["r"][:, :], ALU.mult, ALU.mult).then_inc(s_done, 1)

            def unit_stats(g, p, kind):
                dve.wait_ge(s_ldx[p], g * 16 + 16)
                if kind == 2:
                    v = num(g, p) - NF1
                    for half in range(2):
                        dve.wait_ge(s_yT, v * 2 + 1 + half)
                        dst = xin[:, p, half * HF:(half + 1) * HF]
                        V.tensor_tensor(dst, pt[:, :], dst, ALU.add).then_inc(s_ya, 1)
                    dve.drain()
                stats("ln1", xin[:, p, :], s_mv)

            def unit_refine(u):
                refine("ln1", X_SCALE, s_sd, s_rs, u)

            def low_part(g, p, half):
                u = num(g, p)
                dve.wait_ge(s_xhi, u * 2 + 1 + half)
                hi = xT[:, 0, half * KB:(half + 1) * KB, :].rearrange("p k t -> p (k t)")
                lo = xT[:, 1, half * KB:(half + 1) * KB, :].rearrange("p k t -> p (k t)")
                V.tensor_tensor(lo, pt[:, :], hi, ALU.subtract).then_inc(s_xlo, 1)

            def route(g, p):
                u = num(g, p)
                for nb in range(2):
                    dve.wait_ge(s_sq, u * 2 + 1 + nb)
                    V.tensor_reduce(n2[:, nb * NE // 2:(nb + 1) * NE // 2], sel3[:, nb * NE // 2:(nb + 1) * NE // 2, :],
                                    AX.X, ALU.add)
                dve.drain()
                V.max(top[:, :], n2[:, 0:NE])
                dve.drain()
                V.memset(top[:, TOPK:8], -1.0)
                dve.drain()
                V.match_replace(out=n2m[:, :], in_to_replace=top[:, :], in_values=n2[:, :], imm_value=-1.0)
                dve.drain()
                V.tensor_scalar(mask[:, :], n2m[:, 0:NE], 0.0, None, ALU.is_lt)
                dve.drain()
                V.tensor_tensor(sel3, pv[:, :, :].rearrange("p b (a r) -> p (b a) r", r=R16),
                                mask[:, :].unsqueeze(2).broadcast_to([P, NE, R16]), ALU.mult).then_inc(s_gm, 1)
                dve.drain()
                V.tensor_reduce(vs[:, :], sel[:, :].rearrange("p (a r) -> p r a", r=R16), AX.X, ALU.add)
                dve.drain()
                V.tensor_scalar(vh[:, 0, :], vs[:, :], V_SCALE, None, ALU.mult)
                dve.drain()
                V.scalar_tensor_tensor(vh[:, 1, :], vs[:, :], V_SCALE, vh[:, 0, :], ALU.mult, ALU.subtract)
                for part in range(2):
                    if part:
                        dve.drain()
                    V.tensor_tensor(un[:, part, :, :], mask[:, :].unsqueeze(2).broadcast_to([P, NE, R16]),
                                    vh[:, part, :].unsqueeze(1).broadcast_to([P, NE, R16]), ALU.mult).then_inc(s_u, 1)

            def result(g, p, nb):
                u = num(g, p)
                dve.wait_ge(s_out, u * 2 + 1 + nb)
                dst = xin[:, p, nb * HF:(nb + 1) * HF]
                V.scalar_tensor_tensor(dst, po[:, nb, :], sc[:, 3:4], dst, ALU.mult, ALU.add).then_inc(s_res, 1)

            def delta(q, dt):
                m = q * KD + dt
                s = dt % 2
                dve.wait_ge(s_z, m + 1)
                if dt >= 2:
                    dve.wait_ge(s_dA, q * (4 * NT) + 8 * (dt - 1))
                else:
                    dve.wait_ge(s_dA, q * (4 * NT))
                dve.wait_ge(s_ab, m + 1)
                V.tensor_scalar(dl[:, s, :], pz[:, 0:TC], bdt[:, dt:dt + 1], 0.0, ALU.add, ALU.max).then_inc(s_zm, 1)
                dve.drain()
                dve.wait_ge(s_l, m + 1)
                V.tensor_tensor(dl[:, s, :], dl[:, s, :], lab, ALU.add).then_inc(s_dl, 1)
                dve.drain()
                dve.wait_ge(s_ldt[dt % 3], q * (16 * SLOT_TILES[dt % 3]) + 16 * (dt // 3 + 1))
                dve.wait_ge(s_bu, q * NT + max(2 * dt - 2, 0))
                V.tensor_tensor(dx[:, s, :], dl[:, s, :], xt[:, dt % 3, :], ALU.mult).then_inc(s_dx, 1)

            def scan(q, k):
                dt, h = k // 2, k % 2
                slot = k % 3
                dve.wait_ge(s_bu, q * NT + k + 1)
                for j in range(NH // 2):
                    dve.wait_ge(s_dA, q * (4 * NT) + 4 * k + j + 1)
                    for i in range(2):
                        n = 2 * j + i
                        last = V.tensor_tensor_scan(Tr[:, slot, n, :], pA[:, j % 2, i, :], Tr[:, slot, n, :],
                                                    hst[:, dt, h * NH + n:h * NH + n + 1], ALU.mult, ALU.add)
                    last.then_inc(s_dAf[j % 2], 1)
                dve.drain()
                V.tensor_copy(hst[:, dt, h * NH:(h + 1) * NH], Tr[:, slot, 0:NH, TC - 1]).then_inc(s_h, 1)
                if POOL_C < NH:
                    dve.drain()
                    if dt == 0:
                        dve.wait_ge(s_ldc[h], q * 32 + 32)
                    rest = Tr[:, slot, POOL_C:NH, :]
                    V.tensor_tensor(rest, rest, Cb[:, h * NH + POOL_C:(h + 1) * NH, :], ALU.mult)

            def reduce(q, k):
                dt, h = k // 2, k % 2
                s = dt % 3
                dve.drain()
                dve.wait_ge(s_cm, q * NT + k + 1)
                if h == 0:
                    V.tensor_reduce(Tr[:, (k + 1) % 3, NH, :], Tr[:, k % 3, 0:NH, :].rearrange("p n t -> p t n"),
                                    AX.X, ALU.add).then_inc(s_rd, 1)
                else:
                    V.tensor_reduce(Tr[:, (k + 1) % 3, NH, :], Tr[:, k % 3, :, :].rearrange("p n t -> p t n"),
                                    AX.X, ALU.add)
                    dve.drain()
                    V.scalar_tensor_tensor(xt[:, s, :], xt[:, s, :], Dp[:, dt:dt + 1], Tr[:, (k + 1) % 3, NH, :],
                                           ALU.mult, ALU.add).then_inc(s_y, 1)
                    V.drain().then_inc(s_rd, 1)

            def opening(g, kind):
                unit_stats(g, 0, kind)
                unit_refine(num(g, 0))
                low_part(g, 0, 0)
                low_part(g, 0, 1)

            def between(phase):
                if phase in (1, 2):
                    dve.drain()
                    V.memset(hst[:, :, :], 0.0)
                    dve.drain()

            def pair(g, q, kind, last):
                for p in range(2):
                    u = num(g, p)
                    g2, p2 = after(g, p)
                    more = not (last and p == 1)

                    def half(h):
                        if q is None:
                            return
                        k = p * KD + h
                        scan(q, k)
                        if h % 2 == 0 and k // 2 + 1 < KD:
                            delta(q, k // 2 + 1)
                        if k > 0:
                            reduce(q, k - 1)

                    if q is not None and p == 0:
                        delta(q, 0)
                    route(g, p)
                    if more:
                        unit_stats(g2, p2, kind)
                    half(0)
                    if more:
                        unit_refine(u + 1)
                    half(1)
                    half(2)
                    if more:
                        low_part(g2, p2, 0)
                    result(g, p, 0)
                    half(3)
                    if more:
                        low_part(g2, p2, 1)
                    result(g, p, 1)
                    if kind == 1:
                        dve.drain()
                        stats("ln2", xin[:, p, :], s_mv2)
                    half(4)
                    if kind == 1:
                        refine("ln2", 1.0, s_sd2, s_rs2, u)
                    for h in range(5, 8):
                        half(h)
                if q is not None:
                    reduce(q, NT - 1)

            phases(dve, pair, opening, between)


def kernel(L0_attn_x, L0_attn_W_xproj, L0_attn_W_dt, L0_attn_b_dt, L0_attn_A_log, L0_attn_D_param,
           L0_ffn_A, L0_ffn_B, L0_ffn_W, L0_ffn_bias):
    import numpy as np
    import concourse.bacc as bacc
    from concourse.bass_utils import run_bass_kernel_spmd

    c = np.ascontiguousarray
    x = np.asarray(L0_attn_x)
    D = x.shape[2]
    A, B, W = np.asarray(L0_ffn_A), np.asarray(L0_ffn_B), np.asarray(L0_ffn_W)
    blocks = D // P
    arrays = {
        "x": c(x),
        "AT": c(A.reshape(-1, D).T),
        "BT": c(B.transpose(0, 2, 1).reshape(-1, B.shape[1])),
        "WT": c(W.T),
        "bias": c(np.asarray(L0_ffn_bias).reshape(1, -1)),
        "WxT": c(np.asarray(L0_attn_W_xproj).T),
        "WdtT": c(np.asarray(L0_attn_W_dt).T),
        "b_dt": c(np.asarray(L0_attn_b_dt).reshape(blocks, P).T),
        "A_log": c(np.asarray(L0_attn_A_log).reshape(blocks, P, -1).transpose(1, 0, 2)),
        "D_par": c(np.asarray(L0_attn_D_param).reshape(blocks, P).T),
    }
    nc = bacc.Bacc("TRN2", target_bir_lowering=False, num_devices=1)
    args = [nc.dram_tensor(n, a.shape, mybir.dt.from_np(a.dtype), kind="ExternalInput").ap() for n, a in arrays.items()]
    out = nc.dram_tensor("out", x.shape, mybir.dt.float32, kind="ExternalOutput").ap()
    build(nc, *args, out)
    r = run_bass_kernel_spmd(nc, [arrays], core_ids=[0])
    return r.results[0]["out"]
```

```python
import concourse.bass as bass
from concourse import mybir
from contextlib import ExitStack

P = 128
TC = 256
NH = 8
TOPK = 4
EPS = 1e-5
X_SCALE = 1024.0
V_SCALE = 2.0 ** -21
POOL_C = 8


def build(nc, x, AT, BT, WT, bias, WxT, WdtT, b_dt, A_log, D_par, out):
    f32, f16, bf16, i32 = mybir.dt.float32, mybir.dt.float16, mybir.dt.bfloat16, mybir.dt.int32
    ALU, ACT, AX = mybir.AluOpType, mybir.ActivationFunctionType, mybir.AxisListType
    RMAX = bass.bass_isa.ReduceOp.max

    BSZ, T, D = x.shape
    KD = D // P
    R16 = 16
    NE = AT.shape[1] // R16
    NS = A_log.shape[2]
    RX = WdtT.shape[0]
    NX = WxT.shape[1]
    NTOK = BSZ * T
    UB = T // P
    GB = UB // 2
    NF1 = BSZ * UB
    HF = D // 2
    KB = KD // 2
    NT = 2 * KD
    SLOT_TILES = [len(range(n, KD, 3)) for n in range(3)]

    x_r = x.rearrange("b t d -> (b t) d")
    out_r = out.rearrange("b t d -> (b t) d")
    x2_d = nc.dram_tensor("x2_scratch", (NTOK, D), f32, kind="Internal").ap()
    xnT_d = nc.dram_tensor("xnT_scratch", (NTOK, D), f32, kind="Internal").ap()
    yT_d = nc.dram_tensor("yT_scratch", (NTOK, D), f32, kind="Internal").ap()
    dr_d = nc.dram_tensor("delta_rank_scratch", (NTOK, P), f32, kind="Internal").ap()
    bc_d = nc.dram_tensor("bc_scratch", (NTOK, P), f32, kind="Internal").ap()
    xnT_u = xnT_d.rearrange("(u p) (k t) -> p u k t", p=P, t=P)
    yT_u = yT_d.rearrange("(u p) (k t) -> p u k t", p=P, t=P)
    dr_u = dr_d.rearrange("(u p) t -> p u t", p=P)
    bc_u = bc_d.rearrange("(u n) t -> n u t", n=P)

    ctx = ExitStack()
    with ctx:
        def sb(name, shape, dt=f32):
            return ctx.enter_context(nc.sbuf_tensor(name, shape, dt))

        def sem(name):
            return ctx.enter_context(nc.semaphore(name))

        wA = sb("wA", [P, 2, KD, D], f16)
        wB = sb("wB", [P, 2, KD, D], f16)
        wW = sb("wW", [P, 2, KD, D], f16)
        wx = sb("wx", [P, KD, NX])
        wdt = sb("wdt", [RX, D])
        mreg = sb("mreg", [P, 2 * NS * TC + 3 * (NH + 1) * TC + 9 * TC])
        o = 0
        Bb = mreg[:, o:o + NS * TC].rearrange("p (n t) -> p n t", n=NS); o += NS * TC
        Cb = mreg[:, o:o + NS * TC].rearrange("p (n t) -> p n t", n=NS); o += NS * TC
        Tr = mreg[:, o:o + 3 * (NH + 1) * TC].rearrange("p (s n t) -> p s n t", s=3, n=NH + 1); o += 3 * (NH + 1) * TC
        xt = mreg[:, o:o + 3 * TC].rearrange("p (s t) -> p s t", s=3); o += 3 * TC
        dl = mreg[:, o:o + 2 * TC].rearrange("p (s t) -> p s t", s=2); o += 2 * TC
        dx = mreg[:, o:o + 2 * TC].rearrange("p (s t) -> p s t", s=2); o += 2 * TC
        lab = mreg[:, o:o + TC]; o += TC
        drT = mreg[:, o:o + TC]; o += TC
        stage = [mreg[:, n * KD * D:(n + 1) * KD * D].rearrange("p (k n) -> p k n", k=KD) for n in range(2)]
        xin = sb("xin", [P, 2, D])
        xn = sb("xn", [P, D])
        aux = sb("aux", [P, KD, P])
        auxf = aux[:, :, :].rearrange("p k t -> p (k t)")
        xT = sb("xT", [P, 2, KD, P], f16)
        sel = sb("sel", [P, D])
        sel3 = sel[:, :].rearrange("p (a r) -> p a r", r=R16)
        un = sel[:, :].bitcast(f16).rearrange("p (c a r) -> p c a r", c=2, r=R16)
        un2 = sel[:, :].bitcast(f16).rearrange("p (c k q) -> p c k q", c=2, k=KD)
        uT = sb("uT", [P, 2, KD, P], f16)
        drs = sb("drs", [P, P])
        bcs = sb("bcs", [P, P])
        brow = sb("brow", [P, D], bf16)
        onesb = sb("onesb", [P, P], bf16)
        idf = sb("idf", [P, P])
        idh = sb("idh", [P, P], f16)
        nA = sb("nA", [P, KD, NS])
        hst = sb("hst", [P, KD, NS])
        bdt = sb("bdt", [P, KD])
        Dp = sb("Dp", [P, KD])
        n2 = sb("n2", [P, NE + 4])
        n2m = sb("n2m", [P, NE + 4])
        top = sb("top", [P, 8])
        mask = sb("mask", [P, NE])
        vs = sb("vs", [P, R16])
        vh = sb("vh", [P, 2, R16], f16)
        amx = sb("amx", [P, 4])
        amr = sb("amr", [P, 4])
        sc = sb("sc", [P, 16])
        lnb = {n: {k: sb(f"{n}_{k}", [P, w]) for k, w in
                   (("st", 12), ("mv", 2), ("ve", 1), ("r0", 1), ("t", 1), ("r", 1), ("nm", 1))} for n in ("ln1", "ln2")}

        def pb(name, shape, dt=f32):
            return ctx.enter_context(nc.psum_tensor(name, shape, dt))

        pv = pb("pv", [P, 2, HF])
        po = pb("po", [P, 2, HF])
        pt = pb("pt", [P, HF])
        pA = pb("pA", [P, 2, 2, TC])
        pz = pb("pz", [P, HF])
        pth = pt[:, :].bitcast(f16)

        s_wld = [sem(f"s_wld{n}") for n in range(3)]
        s_cst = sem("s_cst"); s_idz = sem("s_idz"); s_id = sem("s_id"); s_amx = sem("s_amx"); s_amr = sem("s_amr")
        s_scl = sem("s_scl"); s_whi = sem("s_whi"); s_wlo = sem("s_wlo"); s_bp = sem("s_bp"); s_bmv = sem("s_bmv")
        s_nA = sem("s_nA")
        s_set = sem("s_set")
        s_ldx = [sem(f"s_ldx{n}") for n in range(2)]
        s_ldy = sem("s_ldy")
        s_stx = [sem(f"s_stx{n}") for n in range(2)]
        s_stn = sem("s_stn"); s_stp = sem("s_stp")
        s_mv = sem("s_mv"); s_sd = sem("s_sd"); s_rs = sem("s_rs"); s_xn = sem("s_xn")
        s_xT = sem("s_xT"); s_xhi = sem("s_xhi"); s_xlo = sem("s_xlo")
        s_vec = sem("s_vec"); s_sq = sem("s_sq"); s_gm = sem("s_gm"); s_u = sem("s_u"); s_uT = sem("s_uT"); s_uc = sem("s_uc")
        s_base = sem("s_base")
        s_out = sem("s_out"); s_res = sem("s_res")
        s_mv2 = sem("s_mv2"); s_sd2 = sem("s_sd2"); s_rs2 = sem("s_rs2"); s_xn2 = sem("s_xn2")
        s_nT = sem("s_nT"); s_nc = sem("s_nc"); s_pj = sem("s_pj"); s_pc = sem("s_pc")
        s_yT = sem("s_yT"); s_ya = sem("s_ya")
        s_ldr = sem("s_ldr"); s_ldb = [sem(f"s_ldb{n}") for n in range(2)]; s_ldc = [sem(f"s_ldc{n}") for n in range(2)]
        s_ldt = [sem(f"s_ldt{n}") for n in range(3)]; s_sty = [sem(f"s_sty{n}") for n in range(3)]
        s_z = sem("s_z"); s_ab = sem("s_ab"); s_l = sem("s_l"); s_zm = sem("s_zm"); s_dl = sem("s_dl"); s_dx = sem("s_dx")
        s_dA = sem("s_dA"); s_dAf = [sem(f"s_dAf{n}") for n in range(2)]
        s_bu = sem("s_bu"); s_h = sem("s_h"); s_cm = sem("s_cm"); s_rd = sem("s_rd"); s_y = sem("s_y")

        block = ctx.enter_context(nc.Block())

        NPAIR = BSZ * GB

        class Unit:
            def __init__(self, kind, u, h, p, w, fronts, f1_done, q, k0, nk, yc=None):
                self.kind, self.u = kind, u
                self.h, self.p = h, p
                self.w = w
                self.fronts = fronts
                self.f1_done = f1_done
                self.q, self.k0, self.nk = q, k0, nk
                self.yc = yc

            def half_at(self, h):
                if self.q is None or h % (KD // self.nk):
                    return None
                return self.k0 + h // (KD // self.nk)

        def units(i, part):
            if part == "head":
                return [Unit(1, 2 * i + p, i, p, 2 * i + p, 0, 2 * i + p, None if i == 0 else i - 1, p * KD, KD)
                        for p in range(2)]
            if part == "tail":
                v = i - NPAIR
                return [Unit(2, 4 * NPAIR - 4 + 2 * v + p, 2 * NPAIR - 2 + v, p, 2 * (i - 2) + p, 0, NF1,
                             i - 1 if v == 0 else None, p * KD, KD, i - 2) for p in range(2)]
            return [Unit(1, 4 * i - 4 + j, 2 * i - 2 + j // 2, 0, 2 * i + j // 2, 2 * i - 3 + j // 2, 2 * i + j // 2,
                         i - 1, j * KB, KB) if j % 2 == 0 else
                    Unit(2, 4 * i - 4 + j, 2 * i - 2 + j // 2, 1, 2 * i - 4 + j // 2, 0, 2 * i + j // 2 + 1,
                         i - 1, j * KB, KB, i - 2) for j in range(4)]

        def schedule(eng, unit, opening, closing, new_batch=None):
            def step(i, part, part_after):
                us = units(i, part)
                after = us[1:] + ([units(i + 1, part_after)[0]] if part_after else [None])
                for n, (a, b) in enumerate(zip(us, after)):
                    unit(a, b, n == 0)
                closing(i, us[0].q, part != "tail")

            opening(units(0, "head")[0])
            step(0, "head", "head")
            if new_batch:
                new_batch()
            step(1, "head", "full")
            with eng.Fori(2, GB + 1) as i:
                step(i, "full", "full")
            if new_batch:
                new_batch()
            with eng.Fori(GB + 1, NPAIR - 1) as i:
                step(i, "full", "full")
            step(NPAIR - 1, "full", None)
            for i in (NPAIR, NPAIR + 1):
                opening(units(i, "tail")[0])
                step(i, "tail", None)

        @block.sync
        def _(sp):
            sp.dma_start(stage[0], AT.rearrange("(k p) n -> p k n", p=P)).then_inc(s_wld[0], 16)
            sp.dma_start(stage[1], WT.rearrange("(k p) n -> p k n", p=P)).then_inc(s_wld[2], 16)
            sp.dma_start(bdt[:, :], b_dt).then_inc(s_cst, 16)
            sp.dma_start(Dp[:, :], D_par).then_inc(s_cst, 16)
            sp.dma_start(nA[:, :, :], A_log).then_inc(s_cst, 16)
            sp.dma_start(wx[:, :, :], WxT.rearrange("(k p) n -> p k n", p=P)).then_inc(s_cst, 16)
            sp.dma_start(wdt[:, :], WdtT).then_inc(s_cst, 16)
            sp.dma_start(uT[0:1, :, :, :].rearrange("p c k t -> p (c k t)").bitcast(f32), bias).then_inc(s_cst, 16)
            sp.wait_ge(s_whi, 1)
            sp.wait_ge(s_wlo, 1)
            sp.dma_start(stage[0], BT.rearrange("(k p) n -> p k n", p=P)).then_inc(s_wld[1], 16)
            sp.wait_ge(s_bp, 1)
            for n in range(2):
                sp.dma_start(brow[n + 1:n + 2, :], auxf[0:1, n * HF:(n + 1) * HF].bitcast(bf16)).then_inc(s_bmv, 16)

            def pieces(a):
                return a.rearrange("p (u t) -> p u t", t=P)

            def load_unit(a, before):
                row = a.w * P
                sp.wait_ge(s_stx[a.p], a.h * 16)
                if a.kind == 1:
                    sp.dma_start(xin[:, a.p, :], x_r[bass.ds(row, P), :]).then_inc(s_ldx[a.p], 16)
                    return
                sp.dma_start(xin[:, a.p, :], x2_d[bass.ds(row, P), :]).then_inc(s_ldx[a.p], 16)
                sp.wait_ge(s_yT, a.w * 2)
                sp.wait_ge(s_pj, before.f1_done)
                for n in range(3):
                    sp.wait_ge(s_sty[n], a.yc * (16 * SLOT_TILES[n]) + 16 * SLOT_TILES[n])
                sp.dma_start(aux[:, :, :], yT_d[bass.ds(row, P), :].rearrange("p (k t) -> p k t", t=P)).then_inc(s_ldy, 16)

            def load_tile(q, dt, first):
                sp.wait_ge(s_sty[dt % 3], q * (16 * SLOT_TILES[dt % 3]) + 16 * (dt // 3))
                sp.dma_start(pieces(xt[:, dt % 3, :]), xnT_u[:, bass.ds(first, 2), dt, :]).then_inc(s_ldt[dt % 3], 16)

            def store_tile(q, dt, first):
                sp.wait_ge(s_y, q * KD + dt + 1)
                sp.dma_start(yT_u[:, bass.ds(first, 2), dt, :], pieces(xt[:, dt % 3, :])).then_inc(s_sty[dt % 3], 16)

            def spread(q, h, what, first):
                dst, row = (Bb, 0) if what == "b" else (Cb, NS)
                s = (s_ldb if what == "b" else s_ldc)[h]
                for n in range(2):
                    src = bc_u[row + h * NH:row + (h + 1) * NH, bass.ds(first + n, 1), :].rearrange("n u t -> n (u t)")
                    sp.dma_start(dst[:, h * NH:(h + 1) * NH, n * P:(n + 1) * P], src.partition_broadcast(P)).then_inc(s, 16)

            def load_chunk(q):
                first = q * 2
                sp.wait_ge(s_z, q * KD)
                sp.wait_ge(s_stp, q * 64 + 64)
                sp.dma_start(pieces(drT), dr_u[:, bass.ds(first, 2), :]).then_inc(s_ldr, 16)
                for h in range(2):
                    sp.wait_ge(s_bu, q * NT)
                    spread(q, h, "b", first)
                for dt in range(3):
                    load_tile(q, dt, first)
                for h in range(2):
                    sp.wait_ge(s_rd, q * NT)
                    spread(q, h, "c", first)

            def opening(a):
                load_unit(a, a)

            def unit(a, b, first_of_step):
                row = a.w * P
                tiles = [] if a.q is None else [a.k0 // 2 + n - 1 for n in range(a.nk // 2)]

                def move_tiles(some):
                    for dt in some:
                        if dt >= 0:
                            store_tile(a.q, dt, a.q * 2)
                            if dt + 3 < KD:
                                load_tile(a.q, dt + 3, a.q * 2)

                if b:
                    load_unit(b, a)
                move_tiles(tiles[:len(tiles) // 2])
                sp.wait_ge(s_res, a.u * 2 + 2)
                dst = (x2_d if a.kind == 1 else out_r)[bass.ds(row, P), :]
                sp.dma_start(dst, xin[:, a.p, :]).then_inc(s_stx[a.p], 16)
                move_tiles(tiles[len(tiles) // 2:])
                if a.kind == 1:
                    sp.wait_ge(s_nc, a.w * 2 + 2)
                    sp.dma_start(xnT_d[bass.ds(row, P), :], auxf).then_inc(s_stn, 16)
                    sp.wait_ge(s_pc, a.w + 1)
                    sp.dma_start(dr_d[bass.ds(row, P), :], drs[:, :]).then_inc(s_stp, 16)
                    sp.dma_start(bc_d[bass.ds(row, 2 * NS), :], bcs[P - 2 * NS:P, :]).then_inc(s_stp, 16)
                    sp.wait_ge(s_stn, a.w * 16 + 16)

            def closing(i, q, more_chunks):
                if q is not None:
                    store_tile(q, KD - 1, q * 2)
                if more_chunks:
                    load_chunk(i)

            schedule(sp, unit, opening, closing)
            for n in range(2):
                sp.wait_ge(s_stx[n], 16 * NF1)

        @block.gpsimd
        def _(pool):
            pool.memset(idf[:, :], 0.0).then_inc(s_idz, 1)
            pool.memset(idh[:, :], 0.0).then_inc(s_idz, 1)
            pool.wait_ge(s_idz, 2)
            for m in (idf, idh):
                pool.affine_select(out=m[:, :], in_=m[:, :], compare_op=ALU.not_equal, fill=1.0, base=0,
                                   pattern=[[-1, P]], channel_multiplier=1).then_inc(s_id, 1)
            pool.memset(onesb[:, :], 1.0).then_inc(s_id, 1)
            for n in range(3):
                pool.wait_ge(s_amx, n + 1)
                pool.partition_all_reduce(amr[:, n:n + 1], amx[:, n:n + 1], P, RMAX).then_inc(s_amr, 1)

            def times_b(q, k):
                dt, h = k // 2, k % 2
                if k % 2 == 0:
                    pool.wait_ge(s_dx, q * KD + dt + 1)
                if dt == 0:
                    pool.wait_ge(s_ldb[h], q * 32 + 32)
                pool.wait_ge(s_rd, q * NT + max(k - 2, 0))
                dst = Tr[:, k % 3, 0:NH, :]
                pool.tensor_tensor(dst, Bb[:, h * NH:(h + 1) * NH, :],
                                   dx[:, dt % 2, :].unsqueeze(1).broadcast_to([P, NH, TC]), ALU.mult).then_inc(s_bu, 1)

            def times_c(q, k):
                dt, h = k // 2, k % 2
                pool.wait_ge(s_h, q * NT + k + 1)
                if dt == 0:
                    pool.wait_ge(s_ldc[h], q * 32 + 32)
                dst = Tr[:, k % 3, 0:POOL_C, :]
                pool.tensor_tensor(dst, dst, Cb[:, h * NH:h * NH + POOL_C, :], ALU.mult).then_inc(s_cm, 1)

            def chunk(q):
                times_b(q, 0)
                for k in range(NT):
                    if k + 1 < NT:
                        times_b(q, k + 1)
                    times_c(q, k)

            chunk(0)
            with pool.Fori(1, BSZ * GB) as q:
                chunk(q)

        @block.tensor
        def _(pe):
            pe.wait_ge(s_id, 3)

            def blocks(dst, src, sem_done, idt):
                for k in range(KB):
                    last = nc.tensor.transpose(dst[:, k * P:(k + 1) * P], src(k), idt)
                last.then_inc(sem_done, 1)

            def norm_blocks(a, half):
                u = a.u
                if half == 0:
                    pe.wait_ge(s_xn, u + 1)
                else:
                    pe.wait_ge(s_xhi, u * 2 + 1)
                    pe.wait_ge(s_xlo, u * 2 + 1)
                blocks(pt, lambda k: xn[:, (half * KB + k) * P:(half * KB + k + 1) * P], s_xT, idf[:, :])

            def y_blocks(a, half):
                v = a.w
                if half == 0:
                    pe.wait_ge(s_ldy, v * 16 + 16)
                else:
                    pe.wait_ge(s_ya, v * 2 + 1)
                blocks(pt, lambda k: aux[:, half * KB + k, :], s_yT, idf[:, :])

            def product(dst, lhs, w, nb, first, stop):
                for k in range(KD):
                    for n, (la, wb) in enumerate(((0, 0), (0, 1), (1, 0))):
                        last = nc.tensor.matmul(dst, lhs[:, la, k, :], w[:, wb, k, nb * HF:(nb + 1) * HF],
                                                start=(first and k == 0 and n == 0), stop=(stop and k == KD - 1 and n == 2))
                return last

            def experts(a, nb):
                u = a.u
                if nb == 0:
                    pe.wait_ge(s_xhi, u * 2 + 2)
                    pe.wait_ge(s_xlo, u * 2 + 2)
                    pe.wait_ge(s_gm, u)
                product(pv[:, nb, :], xT, wA, nb, True, True).then_inc(s_vec, 1)

            def base(a, nb):
                u = a.u
                pe.wait_ge(s_res, u * 2)
                nc.tensor.matmul(po[:, nb, :], onesb[:, :], brow[:, nb * HF:(nb + 1) * HF], start=True, stop=False)
                product(po[:, nb, :], xT, wW, nb, False, False)

            def routed_blocks(a, part):
                u = a.u
                pe.wait_ge(s_u, u * 2 + 1 + part)
                if part == 1:
                    pe.wait_ge(s_uc, u * 2 + 1)
                for k in range(KD):
                    last = nc.tensor.transpose(pth[:, k * P:(k + 1) * P], un2[:, part, k, :], idh[:, :])
                last.then_inc(s_uT, 1)

            def routed(a, nb):
                u = a.u
                if nb == 0:
                    pe.wait_ge(s_uc, u * 2 + 2)
                product(po[:, nb, :], uT, wB, nb, False, True).then_inc(s_out, 1)

            def scan_inputs(a):
                u = a.w
                pe.wait_ge(s_xn2, u + 1)
                for half in range(2):
                    if half:
                        pe.wait_ge(s_nc, u * 2 + 1)
                    blocks(pt, lambda k: xn[:, (half * KB + k) * P:(half * KB + k + 1) * P], s_nT, idf[:, :])
                pe.wait_ge(s_nc, u * 2 + 2)
                for n, col in enumerate((0, NX - P)):
                    for k in range(KD):
                        last = nc.tensor.matmul(pt[:, n * P:(n + 1) * P], wx[:, k, col:col + P], aux[:, k, :],
                                                start=(k == 0), stop=(k == KD - 1))
                last.then_inc(s_pj, 1)

            def z(q, dt):
                if dt == 0:
                    pe.wait_ge(s_ldr, q * 16 + 16)
                pe.wait_ge(s_ab, q * KD + dt)
                pe.wait_ge(s_zm, q * KD + dt)
                nc.tensor.matmul(pz[:, 0:TC], wdt[:, dt * P:(dt + 1) * P], drT[:, :], start=True, stop=True).then_inc(s_z, 1)

            def opening(a):
                if a.kind == 2:
                    y_blocks(a, 0)
                    y_blocks(a, 1)
                    pe.wait_ge(s_ya, a.w * 2 + 2)
                norm_blocks(a, 0)
                norm_blocks(a, 1)
                for nb in range(2):
                    experts(a, nb)

            def closing(i, q, more_chunks):
                pass

            pe.wait_ge(s_cst, 16 * 6)

            def unit(a, b, first_of_step):
                def z_at(h):
                    k = a.half_at(h)
                    if k is not None and k % 2 == 0 and k // 2 + 1 < KD:
                        z(a.q, k // 2 + 1)

                if a.q is not None and first_of_step:
                    z(a.q, 0)
                base(a, 0)
                pe.wait_ge(s_pc, a.f1_done)
                if b and b.kind == 2:
                    y_blocks(b, 0)
                z_at(0)
                base(a, 1)
                if b and b.kind == 2:
                    y_blocks(b, 1)
                    pe.wait_ge(s_ya, b.w * 2 + 2)
                routed_blocks(a, 0)
                routed_blocks(a, 1)
                routed(a, 0)
                if b:
                    norm_blocks(b, 0)
                z_at(2)
                routed(a, 1)
                if b:
                    norm_blocks(b, 1)
                z_at(4)
                if b:
                    experts(b, 0)
                    experts(b, 1)
                z_at(6)
                if a.kind == 1:
                    scan_inputs(a)

            pe.wait_ge(s_wlo, 3)
            pe.wait_ge(s_whi, 3)
            pe.wait_ge(s_bmv, 32)
            schedule(pe, unit, opening, closing)

        @block.scalar
        def _(act):
            act.preload_act_table_set("natural_log_exp_and_others")
            for n, (w, st, col) in enumerate(((wA, 0, 0), (wB, 0, 1), (wW, 1, 2))):
                act.wait_ge(s_scl, 1 if n == 0 else 2)
                for k in range(KD):
                    last = nc.scalar.activation(w[:, 0, k, :], stage[st][:, k, :], ACT.Identity, scale=sc[:, col:col + 1])
                last.then_inc(s_whi, 1)
            act.wait_ge(s_cst, 16 * 6)
            nc.scalar.activation(nA[:, :, :], nA[:, :, :], ACT.Exp).then_inc(s_nA, 1)

            def seed(ln, s_in, s_done, u):
                b = lnb[ln]
                act.wait_ge(s_in, u + 1)
                nc.scalar.activation(b["r0"][:, :], b["ve"][:, :], ACT.Ln)
                act.drain()
                nc.scalar.activation(b["r0"][:, :], b["r0"][:, :], ACT.Exp, scale=-0.5).then_inc(s_done, 1)

            def normed(a):
                u = a.u
                act.wait_ge(s_rs, u + 1)
                nc.scalar.activation(xn[:, :], xin[:, a.p, :], ACT.Identity, scale=lnb["ln1"]["r"][:, :],
                                     bias=lnb["ln1"]["nm"][:, :]).then_inc(s_xn, 1)

            def high(a, half):
                u = a.u
                act.wait_ge(s_xT, u * 2 + 1 + half)
                nc.scalar.activation(xT[:, 0, half * KB:(half + 1) * KB, :].rearrange("p k t -> p (k t)"), pt[:, :],
                                     ACT.Copy).then_inc(s_xhi, 1)

            def squares(a, nb):
                u = a.u
                act.wait_ge(s_vec, u * 2 + 1 + nb)
                if nb == 0:
                    act.wait_ge(s_uT, u * 2)
                nc.scalar.activation(sel[:, nb * HF:(nb + 1) * HF], pv[:, nb, :], ACT.Square).then_inc(s_sq, 1)

            def routed_copy(a, part):
                u = a.u
                act.wait_ge(s_uT, u * 2 + 1 + part)
                nc.scalar.activation(uT[:, part, :, :].rearrange("p k t -> p (k t)"), pth[:, :], ACT.Copy).then_inc(s_uc, 1)

            def normed2(a):
                u = a.w
                act.wait_ge(s_rs2, u + 1)
                act.wait_ge(s_xn2, u)
                nc.scalar.activation(xn[:, :], xin[:, a.p, :], ACT.Identity, scale=lnb["ln2"]["r"][:, :],
                                     bias=lnb["ln2"]["nm"][:, :]).then_inc(s_xn2, 1)

            def scan_input_copies(a, half):
                u = a.w
                act.wait_ge(s_nT, u * 2 + 1 + half)
                if half == 0:
                    act.wait_ge(s_stn, u * 16)
                    act.wait_ge(s_yT, a.fronts * 2)
                nc.scalar.activation(auxf[:, half * HF:(half + 1) * HF], pt[:, :], ACT.Copy).then_inc(s_nc, 1)

            def projection_copies(a):
                u = a.w
                act.wait_ge(s_pj, u + 1)
                act.wait_ge(s_stp, u * 32)
                nc.scalar.activation(drs[:, :], pt[:, 0:P], ACT.Copy)
                nc.scalar.activation(bcs[P - 2 * NS:P, :], pt[P - 2 * NS:P, P:2 * P], ACT.Copy)
                act.drain().then_inc(s_pc, 1)

            def softplus(q, dt):
                m = q * KD + dt
                act.wait_ge(s_z, m + 1)
                act.wait_ge(s_dl, m)
                nc.scalar.activation(lab, pz[:, 0:TC], ACT.Abs, bias=bdt[:, dt:dt + 1]).then_inc(s_ab, 1)
                act.drain()
                nc.scalar.activation(lab, lab, ACT.Exp, scale=-1.0)
                act.drain()
                nc.scalar.activation(lab, lab, ACT.Ln, bias=1.0).then_inc(s_l, 1)

            def decays(q, k):
                dt, h = k // 2, k % 2
                if h == 0:
                    act.wait_ge(s_dl, q * KD + dt + 1)
                for j in range(NH // 2):
                    act.wait_ge(s_dAf[j % 2], q * (2 * NT) + 2 * k + j // 2)
                    for i in range(2):
                        n = h * NH + 2 * j + i
                        last = nc.scalar.activation(pA[:, j % 2, i, :], dl[:, dt % 2, :], ACT.Exp, scale=nA[:, dt, n:n + 1])
                    last.then_inc(s_dA, 1)

            def opening(a):
                seed("ln1", s_mv, s_sd, a.u)
                normed(a)
                high(a, 0)
                high(a, 1)
                squares(a, 0)
                squares(a, 1)

            def closing(i, q, more_chunks):
                pass

            def new_batch():
                act.wait_ge(s_set, 1)

            def unit(a, b, first_of_step):
                def half(h):
                    k = a.half_at(h)
                    if k is None:
                        return
                    decays(a.q, k)
                    if k % 2 == 0 and k // 2 + 1 < KD:
                        softplus(a.q, k // 2 + 1)

                if a.q is not None and first_of_step:
                    softplus(a.q, 0)
                half(0)
                routed_copy(a, 0)
                routed_copy(a, 1)
                if b:
                    seed("ln1", s_mv, s_sd, b.u)
                half(1)
                if b:
                    normed(b)
                half(2)
                if b:
                    high(b, 0)
                half(3)
                if b:
                    high(b, 1)
                half(4)
                if a.kind == 1:
                    seed("ln2", s_mv2, s_sd2, a.w)
                half(5)
                if a.kind == 1:
                    act.wait_ge(s_xT, a.u * 2 + 4)
                    normed2(a)
                half(6)
                if b:
                    squares(b, 0)
                    squares(b, 1)
                if a.kind == 1:
                    scan_input_copies(a, 0)
                    scan_input_copies(a, 1)
                half(7)
                if a.kind == 1:
                    projection_copies(a)

            schedule(act, unit, opening, closing, new_batch)

        @block.vector
        def _(dve):
            V = nc.vector
            V.memset(sc[:, :], 0.0)
            V.memset(brow[:, :], 0.0)
            V.memset(n2[:, NE:NE + 4], -1.0)
            order = ((0, 0, 0), (1, 0, 1), (2, 1, 2))
            dve.drain()

            def largest(n, st, ld):
                dve.wait_ge(s_wld[ld], 16)
                V.tensor_reduce(amx[:, n:n + 1], stage[st].rearrange("p k n -> p (k n)"), AX.X, ALU.max,
                                apply_absolute_value=True).then_inc(s_amx, 1)

            def power(n):
                dve.wait_ge(s_amr, n + 1)
                V.tensor_scalar(sc[:, 8:9].bitcast(i32), amr[:, n:n + 1].bitcast(i32), 0x7F800000, None, ALU.bitwise_and)
                dve.drain()
                V.tensor_scalar(sc[:, 8:9], sc[:, 8:9], 2.0 ** -40, 2.0 ** 40, ALU.max, ALU.min)
                dve.drain()
                V.reciprocal(sc[:, 9:10], sc[:, 8:9])
                dve.drain()
                V.tensor_scalar(sc[:, 4 + n:5 + n], sc[:, 9:10], 2.0 ** 13, None, ALU.mult)
                dve.drain()

            def low(w, st, col, n):
                dve.wait_ge(s_whi, n + 1)
                for k in range(KD):
                    last = V.scalar_tensor_tensor(w[:, 1, k, :], stage[st][:, k, :], sc[:, col:col + 1], w[:, 0, k, :],
                                                  ALU.mult, ALU.subtract)
                last.then_inc(s_wlo, 1)

            largest(*order[0])
            power(0)
            V.tensor_copy(sc[:, 0:1], sc[:, 4:5]).then_inc(s_scl, 1)
            low(wA, 0, 0, 0)
            largest(*order[1])
            largest(*order[2])
            power(1)
            power(2)
            V.tensor_tensor(sc[:, 10:11], sc[:, 4:5], sc[:, 5:6], ALU.mult)
            dve.drain()
            V.tensor_scalar(sc[:, 10:11], sc[:, 10:11], 2.0 ** -7, None, ALU.mult)
            V.tensor_scalar(sc[:, 11:12], sc[:, 6:7], X_SCALE, None, ALU.mult)
            dve.drain()
            V.tensor_tensor(sc[:, 12:13], sc[:, 10:11], sc[:, 11:12], ALU.min)
            V.reciprocal(sc[:, 13:14], sc[:, 4:5])
            dve.drain()
            V.tensor_scalar(sc[:, 1:2], sc[:, 12:13], sc[:, 13:14], 2.0 ** 7, ALU.mult, ALU.mult)
            V.reciprocal(sc[:, 14:15], sc[:, 12:13])
            V.tensor_scalar(sc[:, 2:3], sc[:, 12:13], 1.0 / X_SCALE, None, ALU.mult).then_inc(s_scl, 1)
            dve.drain()
            V.tensor_scalar(sc[:, 3:4], sc[:, 14:15], 0.5, None, ALU.mult)
            dve.wait_ge(s_cst, 16 * 6)
            brw = uT[0:1, :, :, :].rearrange("p c k t -> p (c k t)").bitcast(f32)
            b2, b3 = (auxf[0:1, n * HF:(n + 1) * HF].bitcast(bf16) for n in range(2))
            V.tensor_scalar(xn[0:1, :], brw, sc[0:1, 12:13], None, ALU.mult)
            dve.drain()
            V.tensor_copy(brow[0:1, :], xn[0:1, :])
            dve.drain()
            V.tensor_tensor(xn[0:1, :], xn[0:1, :], brow[0:1, :], ALU.subtract)
            dve.drain()
            V.tensor_copy(b2, xn[0:1, :])
            dve.drain()
            V.tensor_tensor(xn[0:1, :], xn[0:1, :], b2, ALU.subtract)
            dve.drain()
            V.tensor_copy(b3, xn[0:1, :]).then_inc(s_bp, 1)
            low(wB, 0, 1, 1)
            low(wW, 1, 2, 2)
            dve.wait_ge(s_nA, 1)
            V.tensor_scalar(nA[:, :, :], nA[:, :, :], -1.0, None, ALU.mult).then_inc(s_set, 1)

            def stats(ln, src, s_done):
                b = lnb[ln]
                for n in range(2):
                    V.bn_stats(b["st"][:, 6 * n:6 * n + 6], src[:, n * HF:(n + 1) * HF])
                dve.drain()
                V.bn_aggr(b["mv"][:, :], b["st"][:, :])
                dve.drain()
                V.tensor_scalar(b["ve"][:, :], b["mv"][:, 1:2], EPS, None, ALU.add).then_inc(s_done, 1)

            def refine(ln, scale, s_in, s_done, u):
                b = lnb[ln]
                dve.wait_ge(s_in, u + 1)
                V.scalar_tensor_tensor(b["t"][:, :], b["r0"][:, :], b["ve"][:, :], b["r0"][:, :], ALU.mult, ALU.mult)
                dve.drain()
                V.tensor_scalar(b["t"][:, :], b["t"][:, :], -0.5 * scale, 1.5 * scale, ALU.mult, ALU.add)
                dve.drain()
                V.tensor_tensor(b["r"][:, :], b["r0"][:, :], b["t"][:, :], ALU.mult)
                dve.drain()
                V.scalar_tensor_tensor(b["nm"][:, :], b["mv"][:, 0:1], -1.0, b["r"][:, :], ALU.mult, ALU.mult).then_inc(s_done, 1)

            def unit_stats(a):
                dve.wait_ge(s_ldx[a.p], a.h * 16 + 16)
                if a.kind == 2:
                    v = a.w
                    for half in range(2):
                        dve.wait_ge(s_yT, v * 2 + 1 + half)
                        dst = xin[:, a.p, half * HF:(half + 1) * HF]
                        V.tensor_tensor(dst, pt[:, :], dst, ALU.add).then_inc(s_ya, 1)
                    dve.drain()
                stats("ln1", xin[:, a.p, :], s_mv)

            def unit_refine(u):
                refine("ln1", X_SCALE, s_sd, s_rs, u)

            def low_part(a, half):
                u = a.u
                dve.wait_ge(s_xhi, u * 2 + 1 + half)
                hi = xT[:, 0, half * KB:(half + 1) * KB, :].rearrange("p k t -> p (k t)")
                lo = xT[:, 1, half * KB:(half + 1) * KB, :].rearrange("p k t -> p (k t)")
                V.tensor_tensor(lo, pt[:, :], hi, ALU.subtract).then_inc(s_xlo, 1)

            def route(a):
                u = a.u
                for nb in range(2):
                    dve.wait_ge(s_sq, u * 2 + 1 + nb)
                    V.tensor_reduce(n2[:, nb * NE // 2:(nb + 1) * NE // 2], sel3[:, nb * NE // 2:(nb + 1) * NE // 2, :],
                                    AX.X, ALU.add)
                dve.drain()
                V.max(top[:, :], n2[:, 0:NE])
                dve.drain()
                V.memset(top[:, TOPK:8], -1.0)
                dve.drain()
                V.match_replace(out=n2m[:, :], in_to_replace=top[:, :], in_values=n2[:, :], imm_value=-1.0)
                dve.drain()
                V.tensor_scalar(mask[:, :], n2m[:, 0:NE], 0.0, None, ALU.is_lt)
                dve.drain()
                V.tensor_tensor(sel3, pv[:, :, :].rearrange("p b (a r) -> p (b a) r", r=R16),
                                mask[:, :].unsqueeze(2).broadcast_to([P, NE, R16]), ALU.mult).then_inc(s_gm, 1)
                dve.drain()
                V.tensor_reduce(vs[:, :], sel[:, :].rearrange("p (a r) -> p r a", r=R16), AX.X, ALU.add)
                dve.drain()
                V.tensor_scalar(vh[:, 0, :], vs[:, :], V_SCALE, None, ALU.mult)
                dve.drain()
                V.scalar_tensor_tensor(vh[:, 1, :], vs[:, :], V_SCALE, vh[:, 0, :], ALU.mult, ALU.subtract)
                for part in range(2):
                    if part:
                        dve.drain()
                    V.tensor_tensor(un[:, part, :, :], mask[:, :].unsqueeze(2).broadcast_to([P, NE, R16]),
                                    vh[:, part, :].unsqueeze(1).broadcast_to([P, NE, R16]), ALU.mult).then_inc(s_u, 1)

            def result(a, nb):
                u = a.u
                dve.wait_ge(s_out, u * 2 + 1 + nb)
                dst = xin[:, a.p, nb * HF:(nb + 1) * HF]
                V.scalar_tensor_tensor(dst, po[:, nb, :], sc[:, 3:4], dst, ALU.mult, ALU.add).then_inc(s_res, 1)

            def delta(q, dt):
                m = q * KD + dt
                s = dt % 2
                dve.wait_ge(s_z, m + 1)
                if dt >= 2:
                    dve.wait_ge(s_dA, q * (4 * NT) + 8 * (dt - 1))
                else:
                    dve.wait_ge(s_dA, q * (4 * NT))
                dve.wait_ge(s_ab, m + 1)
                V.tensor_scalar(dl[:, s, :], pz[:, 0:TC], bdt[:, dt:dt + 1], 0.0, ALU.add, ALU.max).then_inc(s_zm, 1)
                dve.drain()
                dve.wait_ge(s_l, m + 1)
                V.tensor_tensor(dl[:, s, :], dl[:, s, :], lab, ALU.add).then_inc(s_dl, 1)
                dve.drain()
                dve.wait_ge(s_ldt[dt % 3], q * (16 * SLOT_TILES[dt % 3]) + 16 * (dt // 3 + 1))
                dve.wait_ge(s_bu, q * NT + max(2 * dt - 2, 0))
                V.tensor_tensor(dx[:, s, :], dl[:, s, :], xt[:, dt % 3, :], ALU.mult).then_inc(s_dx, 1)

            def scan(q, k):
                dt, h = k // 2, k % 2
                slot = k % 3
                dve.wait_ge(s_bu, q * NT + k + 1)
                for j in range(NH // 2):
                    dve.wait_ge(s_dA, q * (4 * NT) + 4 * k + j + 1)
                    for i in range(2):
                        n = 2 * j + i
                        last = V.tensor_tensor_scan(Tr[:, slot, n, :], pA[:, j % 2, i, :], Tr[:, slot, n, :],
                                                    hst[:, dt, h * NH + n:h * NH + n + 1], ALU.mult, ALU.add)
                    last.then_inc(s_dAf[j % 2], 1)
                dve.drain()
                V.tensor_copy(hst[:, dt, h * NH:(h + 1) * NH], Tr[:, slot, 0:NH, TC - 1]).then_inc(s_h, 1)
                if POOL_C < NH:
                    dve.drain()
                    if dt == 0:
                        dve.wait_ge(s_ldc[h], q * 32 + 32)
                    rest = Tr[:, slot, POOL_C:NH, :]
                    V.tensor_tensor(rest, rest, Cb[:, h * NH + POOL_C:(h + 1) * NH, :], ALU.mult)

            def reduce(q, k):
                dt, h = k // 2, k % 2
                s = dt % 3
                if POOL_C < NH:
                    dve.drain()
                dve.wait_ge(s_cm, q * NT + k + 1)
                if h == 0:
                    V.tensor_reduce(Tr[:, (k + 1) % 3, NH, :], Tr[:, k % 3, 0:NH, :].rearrange("p n t -> p t n"),
                                    AX.X, ALU.add).then_inc(s_rd, 1)
                else:
                    V.tensor_reduce(Tr[:, (k + 1) % 3, NH, :], Tr[:, k % 3, :, :].rearrange("p n t -> p t n"),
                                    AX.X, ALU.add)
                    dve.drain()
                    V.scalar_tensor_tensor(xt[:, s, :], xt[:, s, :], Dp[:, dt:dt + 1], Tr[:, (k + 1) % 3, NH, :],
                                           ALU.mult, ALU.add).then_inc(s_y, 1)
                    V.drain().then_inc(s_rd, 1)

            def opening(a):
                unit_stats(a)
                unit_refine(a.u)
                low_part(a, 0)
                low_part(a, 1)

            def new_batch():
                dve.drain()
                V.memset(hst[:, :, :], 0.0)
                dve.drain()

            def closing(i, q, more_chunks):
                if q is not None:
                    dve.drain()
                    reduce(q, NT - 1)

            def unit(a, b, first_of_step):
                def half(h):
                    k = a.half_at(h)
                    if k is None:
                        return
                    scan(a.q, k)
                    if k % 2 == 0 and k // 2 + 1 < KD:
                        delta(a.q, k // 2 + 1)
                    if k > 0:
                        reduce(a.q, k - 1)

                if a.q is not None and first_of_step:
                    delta(a.q, 0)
                route(a)
                if b:
                    unit_stats(b)
                half(0)
                if b:
                    unit_refine(b.u)
                half(1)
                half(2)
                if b:
                    low_part(b, 0)
                result(a, 0)
                half(3)
                if b:
                    low_part(b, 1)
                result(a, 1)
                if a.kind == 1:
                    dve.drain()
                    stats("ln2", xin[:, a.p, :], s_mv2)
                half(4)
                if a.kind == 1:
                    refine("ln2", 1.0, s_sd2, s_rs2, a.w)
                for h in range(5, 8):
                    half(h)

            schedule(dve, unit, opening, closing, new_batch)


def kernel(L0_attn_x, L0_attn_W_xproj, L0_attn_W_dt, L0_attn_b_dt, L0_attn_A_log, L0_attn_D_param,
           L0_ffn_A, L0_ffn_B, L0_ffn_W, L0_ffn_bias):
    import numpy as np
    import concourse.bacc as bacc
    from concourse.bass_utils import run_bass_kernel_spmd

    c = np.ascontiguousarray
    x = np.asarray(L0_attn_x)
    D = x.shape[2]
    A, B, W = np.asarray(L0_ffn_A), np.asarray(L0_ffn_B), np.asarray(L0_ffn_W)
    blocks = D // P
    arrays = {
        "x": c(x),
        "AT": c(A.reshape(-1, D).T),
        "BT": c(B.transpose(0, 2, 1).reshape(-1, B.shape[1])),
        "WT": c(W.T),
        "bias": c(np.asarray(L0_ffn_bias).reshape(1, -1)),
        "WxT": c(np.asarray(L0_attn_W_xproj).T),
        "WdtT": c(np.asarray(L0_attn_W_dt).T),
        "b_dt": c(np.asarray(L0_attn_b_dt).reshape(blocks, P).T),
        "A_log": c(np.asarray(L0_attn_A_log).reshape(blocks, P, -1).transpose(1, 0, 2)),
        "D_par": c(np.asarray(L0_attn_D_param).reshape(blocks, P).T),
    }
    nc = bacc.Bacc("TRN2", target_bir_lowering=False, num_devices=1)
    args = [nc.dram_tensor(n, a.shape, mybir.dt.from_np(a.dtype), kind="ExternalInput").ap() for n, a in arrays.items()]
    out = nc.dram_tensor("out", x.shape, mybir.dt.float32, kind="ExternalOutput").ap()
    build(nc, *args, out)
    r = run_bass_kernel_spmd(nc, [arrays], core_ids=[0])
    return r.results[0]["out"]
```

```python
import concourse.bass as bass
from concourse import mybir
from contextlib import ExitStack

P = 128
TC = 256
NH = 8
TOPK = 4
EPS = 1e-5
X_SCALE = 1024.0
V_SCALE = 2.0 ** -21
POOL_C = 8


def build(nc, x, AT, BT, WT, bias, WxT, WdtT, b_dt, A_log, D_par, out):
    f32, f16, bf16, i32 = mybir.dt.float32, mybir.dt.float16, mybir.dt.bfloat16, mybir.dt.int32
    ALU, ACT, AX = mybir.AluOpType, mybir.ActivationFunctionType, mybir.AxisListType
    RMAX = bass.bass_isa.ReduceOp.max

    BSZ, T, D = x.shape
    KD = D // P
    R16 = 16
    NE = AT.shape[1] // R16
    NS = A_log.shape[2]
    RX = WdtT.shape[0]
    NX = WxT.shape[1]
    NTOK = BSZ * T
    UB = T // P
    GB = UB // 2
    NF1 = BSZ * UB
    HF = D // 2
    KB = KD // 2
    NT = 2 * KD
    SLOT_TILES = [len(range(n, KD, 3)) for n in range(3)]

    x_r = x.rearrange("b t d -> (b t) d")
    out_r = out.rearrange("b t d -> (b t) d")
    x2_d = nc.dram_tensor("x2_scratch", (NTOK, D), f32, kind="Internal").ap()
    xnT_d = nc.dram_tensor("xnT_scratch", (NTOK, D), f32, kind="Internal").ap()
    yT_d = nc.dram_tensor("yT_scratch", (NTOK, D), f32, kind="Internal").ap()
    dr_d = nc.dram_tensor("delta_rank_scratch", (NTOK, P), f32, kind="Internal").ap()
    bc_d = nc.dram_tensor("bc_scratch", (NTOK, P), f32, kind="Internal").ap()
    xnT_u = xnT_d.rearrange("(u p) (k t) -> p u k t", p=P, t=P)
    yT_u = yT_d.rearrange("(u p) (k t) -> p u k t", p=P, t=P)
    dr_u = dr_d.rearrange("(u p) t -> p u t", p=P)
    bc_u = bc_d.rearrange("(u n) t -> n u t", n=P)

    ctx = ExitStack()
    with ctx:
        def sb(name, shape, dt=f32):
            return ctx.enter_context(nc.sbuf_tensor(name, shape, dt))

        def sem(name):
            return ctx.enter_context(nc.semaphore(name))

        wA = sb("wA", [P, 2, KD, D], f16)
        wB = sb("wB", [P, 2, KD, D], f16)
        wW = sb("wW", [P, 2, KD, D], f16)
        wx = sb("wx", [P, KD, NX])
        wdt = sb("wdt", [RX, D])
        mreg = sb("mreg", [P, 2 * NS * TC + 3 * (NH + 1) * TC + 9 * TC])
        o = 0
        Bb = mreg[:, o:o + NS * TC].rearrange("p (n t) -> p n t", n=NS); o += NS * TC
        Cb = mreg[:, o:o + NS * TC].rearrange("p (n t) -> p n t", n=NS); o += NS * TC
        Tr = mreg[:, o:o + 3 * (NH + 1) * TC].rearrange("p (s n t) -> p s n t", s=3, n=NH + 1); o += 3 * (NH + 1) * TC
        xt = mreg[:, o:o + 3 * TC].rearrange("p (s t) -> p s t", s=3); o += 3 * TC
        dl = mreg[:, o:o + 2 * TC].rearrange("p (s t) -> p s t", s=2); o += 2 * TC
        dx = mreg[:, o:o + 2 * TC].rearrange("p (s t) -> p s t", s=2); o += 2 * TC
        lab = mreg[:, o:o + TC]; o += TC
        drT = mreg[:, o:o + TC]; o += TC
        stage = [mreg[:, n * KD * D:(n + 1) * KD * D].rearrange("p (k n) -> p k n", k=KD) for n in range(2)]
        xin = sb("xin", [P, 2, D])
        xn = sb("xn", [P, D])
        aux = sb("aux", [P, KD, P])
        auxf = aux[:, :, :].rearrange("p k t -> p (k t)")
        xT = sb("xT", [P, 2, KD, P], f16)
        sel = sb("sel", [P, D])
        sel3 = sel[:, :].rearrange("p (a r) -> p a r", r=R16)
        un = sel[:, :].bitcast(f16).rearrange("p (c a r) -> p c a r", c=2, r=R16)
        un2 = sel[:, :].bitcast(f16).rearrange("p (c k q) -> p c k q", c=2, k=KD)
        uT = sb("uT", [P, 2, KD, P], f16)
        drs = sb("drs", [P, P])
        bcs = sb("bcs", [P, P])
        brow = sb("brow", [P, D], bf16)
        onesb = sb("onesb", [P, P], bf16)
        idf = sb("idf", [P, P])
        idh = sb("idh", [P, P], f16)
        nA = sb("nA", [P, KD, NS])
        hst = sb("hst", [P, KD, NS])
        bdt = sb("bdt", [P, KD])
        Dp = sb("Dp", [P, KD])
        n2 = sb("n2", [P, NE + 4])
        n2m = sb("n2m", [P, NE + 4])
        top = sb("top", [P, 8])
        mask = sb("mask", [P, NE])
        vs = sb("vs", [P, R16])
        vh = sb("vh", [P, 2, R16], f16)
        amx = sb("amx", [P, 4])
        amr = sb("amr", [P, 4])
        sc = sb("sc", [P, 16])
        lnb = {n: {k: sb(f"{n}_{k}", [P, w]) for k, w in
                   (("st", 12), ("mv", 2), ("ve", 1), ("r0", 1), ("t", 1), ("r", 1), ("nm", 1))} for n in ("ln1", "ln2")}

        def pb(name, shape, dt=f32):
            return ctx.enter_context(nc.psum_tensor(name, shape, dt))

        pv = pb("pv", [P, 2, HF])
        po = pb("po", [P, 2, HF])
        pt = pb("pt", [P, HF])
        pA = pb("pA", [P, 2, 2, TC])
        pz = pb("pz", [P, HF])
        pth = pt[:, :].bitcast(f16)

        s_wld = [sem(f"s_wld{n}") for n in range(3)]
        s_cst = sem("s_cst"); s_idz = sem("s_idz"); s_id = sem("s_id"); s_amx = sem("s_amx"); s_amr = sem("s_amr")
        s_scl = sem("s_scl"); s_whi = sem("s_whi"); s_wlo = sem("s_wlo"); s_bp = sem("s_bp"); s_bmv = sem("s_bmv")
        s_nA = sem("s_nA")
        s_set = sem("s_set")
        s_ldx = [sem(f"s_ldx{n}") for n in range(2)]
        s_ldy = sem("s_ldy")
        s_stx = [sem(f"s_stx{n}") for n in range(2)]
        s_stn = sem("s_stn"); s_stp = sem("s_stp")
        s_mv = sem("s_mv"); s_sd = sem("s_sd"); s_rs = sem("s_rs"); s_xn = sem("s_xn")
        s_xT = sem("s_xT"); s_xhi = sem("s_xhi"); s_xlo = sem("s_xlo")
        s_vec = sem("s_vec"); s_sq = sem("s_sq"); s_gm = sem("s_gm"); s_u = sem("s_u"); s_uT = sem("s_uT"); s_uc = sem("s_uc")
        s_base = sem("s_base")
        s_out = sem("s_out"); s_res = sem("s_res")
        s_mv2 = sem("s_mv2"); s_sd2 = sem("s_sd2"); s_rs2 = sem("s_rs2"); s_xn2 = sem("s_xn2")
        s_nT = sem("s_nT"); s_nc = sem("s_nc"); s_pj = sem("s_pj"); s_pc = sem("s_pc")
        s_yT = sem("s_yT"); s_ya = sem("s_ya")
        s_ldr = sem("s_ldr"); s_ldb = [sem(f"s_ldb{n}") for n in range(2)]; s_ldc = [sem(f"s_ldc{n}") for n in range(2)]
        s_ldt = [sem(f"s_ldt{n}") for n in range(3)]; s_sty = [sem(f"s_sty{n}") for n in range(3)]
        s_z = sem("s_z"); s_ab = sem("s_ab"); s_l = sem("s_l"); s_zm = sem("s_zm"); s_dl = sem("s_dl"); s_dx = sem("s_dx")
        s_dA = sem("s_dA"); s_dAf = [sem(f"s_dAf{n}") for n in range(2)]
        s_bu = sem("s_bu"); s_h = sem("s_h"); s_cm = sem("s_cm"); s_rd = sem("s_rd"); s_y = sem("s_y")

        block = ctx.enter_context(nc.Block())

        NPAIR = BSZ * GB

        class Unit:
            def __init__(self, kind, u, h, p, w, fronts, f1_done, q, k0, nk, yc=None):
                self.kind, self.u = kind, u
                self.h, self.p = h, p
                self.w = w
                self.fronts = fronts
                self.f1_done = f1_done
                self.q, self.k0, self.nk = q, k0, nk
                self.yc = yc
                self.late = None
                self.defers = False
                self.next_chunk = None
                self.y_early = False

            def half_at(self, h):
                if self.q is None or h % (KD // self.nk):
                    return None
                return self.k0 + h // (KD // self.nk)

        def units(i, part):
            if part == "head":
                us = [Unit(1, 2 * i + p, i, p, 2 * i + p, 0, 2 * i + p, None if i == 0 else i - 1, p * KD, KD)
                      for p in range(2)]
                us[1].next_chunk = i
                return us
            if part == "tail":
                v = i - NPAIR
                return [Unit(2, 4 * NPAIR - 4 + 2 * v + p, 2 * NPAIR - 2 + v, p, 2 * (i - 2) + p, 0, NF1,
                             i - 1 if v == 0 else None, p * KD, KD, i - 2) for p in range(2)]
            us = [Unit(1, 4 * i - 4 + j, 2 * i - 2 + j // 2, 0, 2 * i + j // 2, 2 * i - 3 + j // 2, 2 * i + j // 2,
                         i - 1, j * KB, KB) if j % 2 == 0 else
                    Unit(2, 4 * i - 4 + j, 2 * i - 2 + j // 2, 1, 2 * i - 4 + j // 2, 0, 2 * i + j // 2 + 1,
                         i - 1, j * KB, KB, i - 2) for j in range(4)]
            for j in (0, 2):
                us[j].defers, us[j + 1].late = True, us[j]
            us[3].y_early = True
            us[3].next_chunk = i
            return us

        def schedule(eng, unit, opening, closing, new_batch=None):
            def step(i, part, part_after):
                us = units(i, part)
                after = us[1:] + ([units(i + 1, part_after)[0]] if part_after else [None])
                for a, b in zip(us, after):
                    unit(a, b)
                closing(i, us[0].q, part != "tail", part_after == "full")

            opening(units(0, "head")[0])
            step(0, "head", "head")
            if new_batch:
                new_batch()
            step(1, "head", "full")
            with eng.Fori(2, GB + 1) as i:
                step(i, "full", "full")
            if new_batch:
                new_batch()
            with eng.Fori(GB + 1, NPAIR - 1) as i:
                step(i, "full", "full")
            step(NPAIR - 1, "full", None)
            for i in (NPAIR, NPAIR + 1):
                opening(units(i, "tail")[0])
                step(i, "tail", None)

        @block.sync
        def _(sp):
            sp.dma_start(stage[0], AT.rearrange("(k p) n -> p k n", p=P)).then_inc(s_wld[0], 16)
            sp.dma_start(stage[1], WT.rearrange("(k p) n -> p k n", p=P)).then_inc(s_wld[2], 16)
            sp.dma_start(bdt[:, :], b_dt).then_inc(s_cst, 16)
            sp.dma_start(Dp[:, :], D_par).then_inc(s_cst, 16)
            sp.dma_start(nA[:, :, :], A_log).then_inc(s_cst, 16)
            sp.dma_start(wx[:, :, :], WxT.rearrange("(k p) n -> p k n", p=P)).then_inc(s_cst, 16)
            sp.dma_start(wdt[:, :], WdtT).then_inc(s_cst, 16)
            sp.dma_start(uT[0:1, :, :, :].rearrange("p c k t -> p (c k t)").bitcast(f32), bias).then_inc(s_cst, 16)
            sp.wait_ge(s_whi, 1)
            sp.wait_ge(s_wlo, 1)
            sp.dma_start(stage[0], BT.rearrange("(k p) n -> p k n", p=P)).then_inc(s_wld[1], 16)
            sp.wait_ge(s_bp, 1)
            for n in range(2):
                sp.dma_start(brow[n + 1:n + 2, :], auxf[0:1, n * HF:(n + 1) * HF].bitcast(bf16)).then_inc(s_bmv, 16)

            def pieces(a):
                return a.rearrange("p (u t) -> p u t", t=P)

            def load_y(w, yc):
                sp.wait_ge(s_yT, w * 2)
                for n in range(0 if yc is None else 3):
                    sp.wait_ge(s_sty[n], (yc + 1) * (16 * SLOT_TILES[n]))
                src = yT_d[bass.ds(w * P, P), :].rearrange("p (k t) -> p k t", t=P)
                sp.dma_start(aux[:, :, :], src).then_inc(s_ldy, 16)

            def load_unit(a, before):
                row = a.w * P
                if before.late:
                    sp.wait_ge(s_xn2, before.late.w + 1)
                sp.wait_ge(s_stx[a.p], a.h * 16)
                if a.kind == 1:
                    sp.dma_start(xin[:, a.p, :], x_r[bass.ds(row, P), :]).then_inc(s_ldx[a.p], 16)
                    return
                sp.dma_start(xin[:, a.p, :], x2_d[bass.ds(row, P), :]).then_inc(s_ldx[a.p], 16)
                if before.kind == 2:
                    load_y(a.w, a.yc)

            def load_tile(q, dt, first):
                sp.wait_ge(s_sty[dt % 3], q * (16 * SLOT_TILES[dt % 3]) + 16 * (dt // 3))
                sp.dma_start(pieces(xt[:, dt % 3, :]), xnT_u[:, bass.ds(first, 2), dt, :]).then_inc(s_ldt[dt % 3], 16)

            def store_tile(q, dt, first):
                sp.wait_ge(s_y, q * KD + dt + 1)
                sp.dma_start(yT_u[:, bass.ds(first, 2), dt, :], pieces(xt[:, dt % 3, :])).then_inc(s_sty[dt % 3], 16)

            def spread(q, h, what, first):
                dst, row = (Bb, 0) if what == "b" else (Cb, NS)
                s = (s_ldb if what == "b" else s_ldc)[h]
                for n in range(2):
                    src = bc_u[row + h * NH:row + (h + 1) * NH, bass.ds(first + n, 1), :].rearrange("n u t -> n (u t)")
                    sp.dma_start(dst[:, h * NH:(h + 1) * NH, n * P:(n + 1) * P], src.partition_broadcast(P)).then_inc(s, 16)

            def load_ranks(q):
                first = q * 2
                sp.wait_ge(s_z, q * KD)
                sp.wait_ge(s_stp, q * 64 + 64)
                sp.dma_start(pieces(drT), dr_u[:, bass.ds(first, 2), :]).then_inc(s_ldr, 16)

            def load_chunk(q):
                first = q * 2
                load_tile(q, 0, first)
                for h in range(2):
                    sp.wait_ge(s_bu, q * NT)
                    spread(q, h, "b", first)
                load_tile(q, 2, first)

            def load_c(q):
                for h in range(2):
                    sp.wait_ge(s_rd, q * NT)
                    spread(q, h, "c", q * 2)

            def opening(a):
                load_unit(a, a)

            def store_scan_inputs(a):
                row = a.w * P
                sp.wait_ge(s_nc, a.w * 2 + 2)
                sp.dma_start(xnT_d[bass.ds(row, P), :], auxf).then_inc(s_stn, 16)
                sp.wait_ge(s_pc, a.w + 1)
                sp.wait_ge(s_stn, a.w * 16 + 16)
                sp.dma_start(dr_d[bass.ds(row, P), :], drs[:, :]).then_inc(s_stp, 16)
                sp.dma_start(bc_d[bass.ds(row, 2 * NS), :], bcs[P - 2 * NS:P, :]).then_inc(s_stp, 16)

            def unit(a, b):
                tiles = [] if a.q is None else [a.k0 // 2 + n - 1 for n in range(a.nk // 2)]

                def move_tiles(some):
                    for dt in some:
                        if dt >= 0:
                            store_tile(a.q, dt, a.q * 2)
                            if dt + 3 < KD:
                                load_tile(a.q, dt + 3, a.q * 2)

                if b:
                    load_unit(b, a)
                if a.q is not None and a.k0 == 0:
                    load_c(a.q)
                move_tiles(tiles[:len(tiles) // 2])
                if a.late:
                    store_scan_inputs(a.late)
                    if not a.y_early:
                        load_y(a.w + 1, None)
                sp.wait_ge(s_res, a.u * 2 + 2)
                dst = (x2_d if a.kind == 1 else out_r)[bass.ds(a.w * P, P), :]
                sp.dma_start(dst, xin[:, a.p, :]).then_inc(s_stx[a.p], 16)
                if a.next_chunk is not None and a.late:
                    load_ranks(a.next_chunk)
                move_tiles(tiles[len(tiles) // 2:])
                if a.kind == 1 and not a.defers:
                    store_scan_inputs(a)
                    if a.next_chunk is not None:
                        load_ranks(a.next_chunk)

            def closing(i, q, more_chunks, next_y):
                if more_chunks:
                    load_chunk(i)
                if q is not None:
                    store_tile(q, KD - 1, q * 2)
                if more_chunks:
                    load_tile(i, 1, i * 2)
                if next_y:
                    load_y(i * 2 - 2, None)

            schedule(sp, unit, opening, closing)
            for n in range(2):
                sp.wait_ge(s_stx[n], 16 * NF1)

        @block.gpsimd
        def _(pool):
            pool.memset(idf[:, :], 0.0).then_inc(s_idz, 1)
            pool.memset(idh[:, :], 0.0).then_inc(s_idz, 1)
            pool.wait_ge(s_idz, 2)
            for m in (idf, idh):
                pool.affine_select(out=m[:, :], in_=m[:, :], compare_op=ALU.not_equal, fill=1.0, base=0,
                                   pattern=[[-1, P]], channel_multiplier=1).then_inc(s_id, 1)
            pool.memset(onesb[:, :], 1.0).then_inc(s_id, 1)
            for n in range(3):
                pool.wait_ge(s_amx, n + 1)
                pool.partition_all_reduce(amr[:, n:n + 1], amx[:, n:n + 1], P, RMAX).then_inc(s_amr, 1)

            def times_b(q, k):
                dt, h = k // 2, k % 2
                if k % 2 == 0:
                    pool.wait_ge(s_dx, q * KD + dt + 1)
                if dt == 0:
                    pool.wait_ge(s_ldb[h], q * 32 + 32)
                pool.wait_ge(s_rd, q * NT + max(k - 2, 0))
                dst = Tr[:, k % 3, 0:NH, :]
                pool.tensor_tensor(dst, Bb[:, h * NH:(h + 1) * NH, :],
                                   dx[:, dt % 2, :].unsqueeze(1).broadcast_to([P, NH, TC]), ALU.mult).then_inc(s_bu, 1)

            def times_c(q, k):
                dt, h = k // 2, k % 2
                pool.wait_ge(s_h, q * NT + k + 1)
                if dt == 0:
                    pool.wait_ge(s_ldc[h], q * 32 + 32)
                dst = Tr[:, k % 3, 0:POOL_C, :]
                pool.tensor_tensor(dst, dst, Cb[:, h * NH:h * NH + POOL_C, :], ALU.mult).then_inc(s_cm, 1)

            def chunk(q):
                times_b(q, 0)
                for k in range(NT):
                    if k + 1 < NT:
                        times_b(q, k + 1)
                    times_c(q, k)

            chunk(0)
            with pool.Fori(1, BSZ * GB) as q:
                chunk(q)

        @block.tensor
        def _(pe):
            pe.wait_ge(s_id, 3)

            def blocks(dst, src, sem_done, idt):
                for k in range(KB):
                    last = nc.tensor.transpose(dst[:, k * P:(k + 1) * P], src(k), idt)
                last.then_inc(sem_done, 1)

            def norm_blocks(a, half):
                u = a.u
                if half == 0:
                    pe.wait_ge(s_xn, u + 1)
                else:
                    pe.wait_ge(s_xhi, u * 2 + 1)
                    pe.wait_ge(s_xlo, u * 2 + 1)
                blocks(pt, lambda k: xn[:, (half * KB + k) * P:(half * KB + k + 1) * P], s_xT, idf[:, :])

            def y_blocks(a, half):
                v = a.w
                if half == 0:
                    pe.wait_ge(s_ldy, v * 16 + 16)
                else:
                    pe.wait_ge(s_ya, v * 2 + 1)
                blocks(pt, lambda k: aux[:, half * KB + k, :], s_yT, idf[:, :])

            def product(dst, lhs, w, nb, first, stop, between=None):
                for k in range(KD):
                    if between and k == KB:
                        between()
                    for n, (la, wb) in enumerate(((0, 0), (0, 1), (1, 0))):
                        last = nc.tensor.matmul(dst, lhs[:, la, k, :], w[:, wb, k, nb * HF:(nb + 1) * HF],
                                                start=(first and k == 0 and n == 0), stop=(stop and k == KD - 1 and n == 2))
                return last

            def experts(a, nb):
                u = a.u
                if nb == 0:
                    pe.wait_ge(s_xhi, u * 2 + 2)
                    pe.wait_ge(s_xlo, u * 2 + 2)
                    pe.wait_ge(s_gm, u)
                product(pv[:, nb, :], xT, wA, nb, True, True).then_inc(s_vec, 1)

            def base(a, nb, between=None):
                u = a.u
                pe.wait_ge(s_res, u * 2)
                nc.tensor.matmul(po[:, nb, :], onesb[:, :], brow[:, nb * HF:(nb + 1) * HF], start=True, stop=False)
                product(po[:, nb, :], xT, wW, nb, False, False, between)

            def routed_blocks(a, part):
                u = a.u
                pe.wait_ge(s_u, u * 2 + 1 + part)
                if part == 1:
                    pe.wait_ge(s_uc, u * 2 + 1)
                for k in range(KD):
                    last = nc.tensor.transpose(pth[:, k * P:(k + 1) * P], un2[:, part, k, :], idh[:, :])
                last.then_inc(s_uT, 1)

            def routed(a, nb):
                u = a.u
                if nb == 0:
                    pe.wait_ge(s_uc, u * 2 + 2)
                product(po[:, nb, :], uT, wB, nb, False, True).then_inc(s_out, 1)

            def scan_blocks(a, half):
                if half == 0:
                    pe.wait_ge(s_xn2, a.w + 1)
                else:
                    pe.wait_ge(s_nc, a.w * 2 + 1)
                blocks(pt, lambda k: xn[:, (half * KB + k) * P:(half * KB + k + 1) * P], s_nT, idf[:, :])

            def scan_products(a):
                pe.wait_ge(s_nc, a.w * 2 + 2)
                for n, col in enumerate((0, NX - P)):
                    for k in range(KD):
                        last = nc.tensor.matmul(pt[:, n * P:(n + 1) * P], wx[:, k, col:col + P], aux[:, k, :],
                                                start=(k == 0), stop=(k == KD - 1))
                last.then_inc(s_pj, 1)

            def z(q, dt):
                if dt == 0:
                    pe.wait_ge(s_ldr, q * 16 + 16)
                pe.wait_ge(s_ab, q * KD + dt)
                pe.wait_ge(s_zm, q * KD + dt)
                nc.tensor.matmul(pz[:, 0:TC], wdt[:, dt * P:(dt + 1) * P], drT[:, :], start=True, stop=True).then_inc(s_z, 1)

            def opening(a):
                if a.kind == 2:
                    y_blocks(a, 0)
                    y_blocks(a, 1)
                    pe.wait_ge(s_ya, a.w * 2 + 2)
                norm_blocks(a, 0)
                norm_blocks(a, 1)
                for nb in range(2):
                    experts(a, nb)

            def closing(i, q, more_chunks, next_y):
                if more_chunks:
                    z(i, 0)

            pe.wait_ge(s_cst, 16 * 6)

            def unit(a, b):
                def z_at(h):
                    k = a.half_at(h)
                    if k is not None and k % 2 == 0 and k // 2 + 1 < KD:
                        z(a.q, k // 2 + 1)

                if b and b.y_early:
                    y_blocks(b, 0)
                base(a, 0, (lambda: scan_blocks(a.late, 0)) if a.late else None)
                z_at(0)
                if a.late:
                    scan_blocks(a.late, 1)
                if b and b.y_early:
                    y_blocks(b, 1)
                base(a, 1)
                if a.late:
                    scan_products(a.late)
                pe.wait_ge(s_pc, a.f1_done)
                late_y = b and b.kind == 2 and not b.y_early
                if late_y:
                    y_blocks(b, 0)
                if b and b.kind == 2:
                    pe.wait_ge(s_ya, b.w * 2 + (1 if late_y else 2))
                routed_blocks(a, 0)
                routed_blocks(a, 1)
                if late_y:
                    pe.wait_ge(s_uc, a.u * 2 + 2)
                    y_blocks(b, 1)
                routed(a, 0)
                if late_y:
                    pe.wait_ge(s_ya, b.w * 2 + 2)
                if b:
                    norm_blocks(b, 0)
                z_at(2)
                routed(a, 1)
                if b:
                    norm_blocks(b, 1)
                z_at(4)
                if b:
                    experts(b, 0)
                    experts(b, 1)
                z_at(6)
                if a.kind == 1 and not a.defers:
                    scan_blocks(a, 0)
                    scan_blocks(a, 1)
                    scan_products(a)

            pe.wait_ge(s_wlo, 3)
            pe.wait_ge(s_whi, 3)
            pe.wait_ge(s_bmv, 32)
            schedule(pe, unit, opening, closing)

        @block.scalar
        def _(act):
            act.preload_act_table_set("natural_log_exp_and_others")
            for n, (w, st, col) in enumerate(((wA, 0, 0), (wB, 0, 1), (wW, 1, 2))):
                act.wait_ge(s_scl, 1 if n == 0 else 2)
                for k in range(KD):
                    last = nc.scalar.activation(w[:, 0, k, :], stage[st][:, k, :], ACT.Identity, scale=sc[:, col:col + 1])
                last.then_inc(s_whi, 1)
            act.wait_ge(s_cst, 16 * 6)
            nc.scalar.activation(nA[:, :, :], nA[:, :, :], ACT.Exp).then_inc(s_nA, 1)

            def seed(ln, s_in, s_done, u):
                b = lnb[ln]
                act.wait_ge(s_in, u + 1)
                nc.scalar.activation(b["r0"][:, :], b["ve"][:, :], ACT.Ln)
                act.drain()
                nc.scalar.activation(b["r0"][:, :], b["r0"][:, :], ACT.Exp, scale=-0.5).then_inc(s_done, 1)

            def normed(a):
                u = a.u
                act.wait_ge(s_rs, u + 1)
                nc.scalar.activation(xn[:, :], xin[:, a.p, :], ACT.Identity, scale=lnb["ln1"]["r"][:, :],
                                     bias=lnb["ln1"]["nm"][:, :]).then_inc(s_xn, 1)

            def high(a, half):
                u = a.u
                act.wait_ge(s_xT, u * 2 + 1 + half)
                nc.scalar.activation(xT[:, 0, half * KB:(half + 1) * KB, :].rearrange("p k t -> p (k t)"), pt[:, :],
                                     ACT.Copy).then_inc(s_xhi, 1)

            def squares(a, nb):
                u = a.u
                act.wait_ge(s_vec, u * 2 + 1 + nb)
                if nb == 0:
                    act.wait_ge(s_uT, u * 2)
                nc.scalar.activation(sel[:, nb * HF:(nb + 1) * HF], pv[:, nb, :], ACT.Square).then_inc(s_sq, 1)

            def routed_copy(a, part):
                u = a.u
                act.wait_ge(s_uT, u * 2 + 1 + part)
                nc.scalar.activation(uT[:, part, :, :].rearrange("p k t -> p (k t)"), pth[:, :], ACT.Copy).then_inc(s_uc, 1)

            def normed2(a):
                u = a.w
                act.wait_ge(s_rs2, u + 1)
                act.wait_ge(s_xn2, u)
                nc.scalar.activation(xn[:, :], xin[:, a.p, :], ACT.Identity, scale=lnb["ln2"]["r"][:, :],
                                     bias=lnb["ln2"]["nm"][:, :]).then_inc(s_xn2, 1)

            def scan_input_copies(a, half):
                u = a.w
                act.wait_ge(s_nT, u * 2 + 1 + half)
                if half == 0:
                    act.wait_ge(s_stn, u * 16)
                    act.wait_ge(s_yT, a.fronts * 2)
                nc.scalar.activation(auxf[:, half * HF:(half + 1) * HF], pt[:, :], ACT.Copy).then_inc(s_nc, 1)

            def projection_copies(a):
                u = a.w
                act.wait_ge(s_pj, u + 1)
                act.wait_ge(s_stp, u * 32)
                nc.scalar.activation(drs[:, :], pt[:, 0:P], ACT.Copy)
                nc.scalar.activation(bcs[P - 2 * NS:P, :], pt[P - 2 * NS:P, P:2 * P], ACT.Copy)
                act.drain().then_inc(s_pc, 1)

            def softplus(q, dt):
                m = q * KD + dt
                act.wait_ge(s_z, m + 1)
                act.wait_ge(s_dl, m)
                nc.scalar.activation(lab, pz[:, 0:TC], ACT.Abs, bias=bdt[:, dt:dt + 1]).then_inc(s_ab, 1)
                act.drain()
                nc.scalar.activation(lab, lab, ACT.Exp, scale=-1.0)
                act.drain()
                nc.scalar.activation(lab, lab, ACT.Ln, bias=1.0).then_inc(s_l, 1)

            def decays(q, k, banks=range(NH // 2)):
                dt, h = k // 2, k % 2
                if h == 0 and 0 in banks:
                    act.wait_ge(s_dl, q * KD + dt + 1)
                for j in banks:
                    act.wait_ge(s_dAf[j % 2], q * (2 * NT) + 2 * k + j // 2)
                    for i in range(2):
                        n = h * NH + 2 * j + i
                        last = nc.scalar.activation(pA[:, j % 2, i, :], dl[:, dt % 2, :], ACT.Exp, scale=nA[:, dt, n:n + 1])
                    last.then_inc(s_dA, 1)

            def opening(a):
                seed("ln1", s_mv, s_sd, a.u)
                normed(a)
                high(a, 0)
                high(a, 1)
                squares(a, 0)
                squares(a, 1)

            def closing(i, q, more_chunks, next_y):
                if more_chunks:
                    softplus(i, 0)

            def new_batch():
                act.wait_ge(s_set, 1)

            def unit(a, b):
                def first_banks(h):
                    if a.half_at(h) is not None:
                        decays(a.q, a.half_at(h), (0, 1))

                def half(h):
                    k = a.half_at(h)
                    if k is None:
                        return
                    decays(a.q, k, range(2 if h in (0, 2) else 0, NH // 2))
                    if k % 2 == 0 and k // 2 + 1 < KD:
                        softplus(a.q, k // 2 + 1)

                if a.late:
                    scan_input_copies(a.late, 0)
                    scan_input_copies(a.late, 1)
                first_banks(0)
                if a.late:
                    projection_copies(a.late)
                routed_copy(a, 0)
                routed_copy(a, 1)
                half(0)
                if b:
                    seed("ln1", s_mv, s_sd, b.u)
                half(1)
                first_banks(2)
                if b:
                    normed(b)
                half(2)
                if b:
                    high(b, 0)
                half(3)
                if b:
                    high(b, 1)
                if a.kind == 1:
                    seed("ln2", s_mv2, s_sd2, a.w)
                half(4)
                half(5)
                if a.kind == 1:
                    act.wait_ge(s_xT, a.u * 2 + 4)
                    normed2(a)
                half(6)
                if b:
                    squares(b, 0)
                    squares(b, 1)
                if a.kind == 1 and not a.defers:
                    scan_input_copies(a, 0)
                    scan_input_copies(a, 1)
                half(7)
                if a.kind == 1 and not a.defers:
                    projection_copies(a)

            schedule(act, unit, opening, closing, new_batch)

        @block.vector
        def _(dve):
            V = nc.vector
            V.memset(sc[:, :], 0.0)
            V.memset(brow[:, :], 0.0)
            V.memset(n2[:, NE:NE + 4], -1.0)
            order = ((0, 0, 0), (1, 0, 1), (2, 1, 2))
            dve.drain()

            def largest(n, st, ld):
                dve.wait_ge(s_wld[ld], 16)
                V.tensor_reduce(amx[:, n:n + 1], stage[st].rearrange("p k n -> p (k n)"), AX.X, ALU.max,
                                apply_absolute_value=True).then_inc(s_amx, 1)

            def power(n):
                dve.wait_ge(s_amr, n + 1)
                V.tensor_scalar(sc[:, 8:9].bitcast(i32), amr[:, n:n + 1].bitcast(i32), 0x7F800000, None, ALU.bitwise_and)
                dve.drain()
                V.tensor_scalar(sc[:, 8:9], sc[:, 8:9], 2.0 ** -40, 2.0 ** 40, ALU.max, ALU.min)
                dve.drain()
                V.reciprocal(sc[:, 9:10], sc[:, 8:9])
                dve.drain()
                V.tensor_scalar(sc[:, 4 + n:5 + n], sc[:, 9:10], 2.0 ** 13, None, ALU.mult)
                dve.drain()

            def low(w, st, col, n):
                dve.wait_ge(s_whi, n + 1)
                for k in range(KD):
                    last = V.scalar_tensor_tensor(w[:, 1, k, :], stage[st][:, k, :], sc[:, col:col + 1], w[:, 0, k, :],
                                                  ALU.mult, ALU.subtract)
                last.then_inc(s_wlo, 1)

            largest(*order[0])
            power(0)
            V.tensor_copy(sc[:, 0:1], sc[:, 4:5]).then_inc(s_scl, 1)
            low(wA, 0, 0, 0)
            largest(*order[1])
            largest(*order[2])
            power(1)
            power(2)
            V.tensor_tensor(sc[:, 10:11], sc[:, 4:5], sc[:, 5:6], ALU.mult)
            dve.drain()
            V.tensor_scalar(sc[:, 10:11], sc[:, 10:11], 2.0 ** -7, None, ALU.mult)
            V.tensor_scalar(sc[:, 11:12], sc[:, 6:7], X_SCALE, None, ALU.mult)
            dve.drain()
            V.tensor_tensor(sc[:, 12:13], sc[:, 10:11], sc[:, 11:12], ALU.min)
            V.reciprocal(sc[:, 13:14], sc[:, 4:5])
            dve.drain()
            V.tensor_scalar(sc[:, 1:2], sc[:, 12:13], sc[:, 13:14], 2.0 ** 7, ALU.mult, ALU.mult)
            V.reciprocal(sc[:, 14:15], sc[:, 12:13])
            V.tensor_scalar(sc[:, 2:3], sc[:, 12:13], 1.0 / X_SCALE, None, ALU.mult).then_inc(s_scl, 1)
            dve.drain()
            V.tensor_scalar(sc[:, 3:4], sc[:, 14:15], 0.5, None, ALU.mult)
            dve.wait_ge(s_cst, 16 * 6)
            brw = uT[0:1, :, :, :].rearrange("p c k t -> p (c k t)").bitcast(f32)
            b2, b3 = (auxf[0:1, n * HF:(n + 1) * HF].bitcast(bf16) for n in range(2))
            V.tensor_scalar(xn[0:1, :], brw, sc[0:1, 12:13], None, ALU.mult)
            dve.drain()
            V.tensor_copy(brow[0:1, :], xn[0:1, :])
            dve.drain()
            V.tensor_tensor(xn[0:1, :], xn[0:1, :], brow[0:1, :], ALU.subtract)
            dve.drain()
            V.tensor_copy(b2, xn[0:1, :])
            dve.drain()
            V.tensor_tensor(xn[0:1, :], xn[0:1, :], b2, ALU.subtract)
            dve.drain()
            V.tensor_copy(b3, xn[0:1, :]).then_inc(s_bp, 1)
            low(wB, 0, 1, 1)
            low(wW, 1, 2, 2)
            dve.wait_ge(s_nA, 1)
            V.tensor_scalar(nA[:, :, :], nA[:, :, :], -1.0, None, ALU.mult).then_inc(s_set, 1)

            def stats(ln, src, s_done):
                b = lnb[ln]
                for n in range(2):
                    V.bn_stats(b["st"][:, 6 * n:6 * n + 6], src[:, n * HF:(n + 1) * HF])
                dve.drain()
                V.bn_aggr(b["mv"][:, :], b["st"][:, :])
                dve.drain()
                V.tensor_scalar(b["ve"][:, :], b["mv"][:, 1:2], EPS, None, ALU.add).then_inc(s_done, 1)

            def refine(ln, scale, s_in, s_done, u):
                b = lnb[ln]
                dve.wait_ge(s_in, u + 1)
                V.scalar_tensor_tensor(b["t"][:, :], b["r0"][:, :], b["ve"][:, :], b["r0"][:, :], ALU.mult, ALU.mult)
                dve.drain()
                V.tensor_scalar(b["t"][:, :], b["t"][:, :], -0.5 * scale, 1.5 * scale, ALU.mult, ALU.add)
                dve.drain()
                V.tensor_tensor(b["r"][:, :], b["r0"][:, :], b["t"][:, :], ALU.mult)
                dve.drain()
                V.scalar_tensor_tensor(b["nm"][:, :], b["mv"][:, 0:1], -1.0, b["r"][:, :], ALU.mult, ALU.mult).then_inc(s_done, 1)

            def add_y(a, half):
                if half == 0:
                    dve.wait_ge(s_ldx[a.p], a.h * 16 + 16)
                dve.wait_ge(s_yT, a.w * 2 + 1 + half)
                dst = xin[:, a.p, half * HF:(half + 1) * HF]
                V.tensor_tensor(dst, pt[:, :], dst, ALU.add).then_inc(s_ya, 1)

            def unit_stats(a):
                if a.kind == 1:
                    dve.wait_ge(s_ldx[a.p], a.h * 16 + 16)
                else:
                    add_y(a, 1)
                    dve.drain()
                stats("ln1", xin[:, a.p, :], s_mv)

            def unit_refine(u):
                refine("ln1", X_SCALE, s_sd, s_rs, u)

            def low_part(a, half):
                u = a.u
                dve.wait_ge(s_xhi, u * 2 + 1 + half)
                hi = xT[:, 0, half * KB:(half + 1) * KB, :].rearrange("p k t -> p (k t)")
                lo = xT[:, 1, half * KB:(half + 1) * KB, :].rearrange("p k t -> p (k t)")
                V.tensor_tensor(lo, pt[:, :], hi, ALU.subtract).then_inc(s_xlo, 1)

            def route(a):
                u = a.u
                for nb in range(2):
                    dve.wait_ge(s_sq, u * 2 + 1 + nb)
                    V.tensor_reduce(n2[:, nb * NE // 2:(nb + 1) * NE // 2], sel3[:, nb * NE // 2:(nb + 1) * NE // 2, :],
                                    AX.X, ALU.add)
                dve.drain()
                V.max(top[:, :], n2[:, 0:NE])
                dve.drain()
                V.memset(top[:, TOPK:8], -1.0)
                dve.drain()
                V.match_replace(out=n2m[:, :], in_to_replace=top[:, :], in_values=n2[:, :], imm_value=-1.0)
                dve.drain()
                V.tensor_scalar(mask[:, :], n2m[:, 0:NE], 0.0, None, ALU.is_lt)
                dve.drain()
                V.tensor_tensor(sel3, pv[:, :, :].rearrange("p b (a r) -> p (b a) r", r=R16),
                                mask[:, :].unsqueeze(2).broadcast_to([P, NE, R16]), ALU.mult).then_inc(s_gm, 1)
                dve.drain()
                V.tensor_reduce(vs[:, :], sel[:, :].rearrange("p (a r) -> p r a", r=R16), AX.X, ALU.add)
                dve.drain()
                V.tensor_scalar(vh[:, 0, :], vs[:, :], V_SCALE, None, ALU.mult)
                dve.drain()
                V.scalar_tensor_tensor(vh[:, 1, :], vs[:, :], V_SCALE, vh[:, 0, :], ALU.mult, ALU.subtract)
                for part in range(2):
                    if part:
                        dve.drain()
                    V.tensor_tensor(un[:, part, :, :], mask[:, :].unsqueeze(2).broadcast_to([P, NE, R16]),
                                    vh[:, part, :].unsqueeze(1).broadcast_to([P, NE, R16]), ALU.mult).then_inc(s_u, 1)

            def result(a, nb):
                u = a.u
                dve.wait_ge(s_out, u * 2 + 1 + nb)
                dst = xin[:, a.p, nb * HF:(nb + 1) * HF]
                V.scalar_tensor_tensor(dst, po[:, nb, :], sc[:, 3:4], dst, ALU.mult, ALU.add).then_inc(s_res, 1)

            def delta(q, dt):
                m = q * KD + dt
                s = dt % 2
                dve.wait_ge(s_z, m + 1)
                if dt >= 2:
                    dve.wait_ge(s_dA, q * (4 * NT) + 8 * (dt - 1))
                else:
                    dve.wait_ge(s_dA, q * (4 * NT))
                dve.wait_ge(s_ab, m + 1)
                V.tensor_scalar(dl[:, s, :], pz[:, 0:TC], bdt[:, dt:dt + 1], 0.0, ALU.add, ALU.max).then_inc(s_zm, 1)
                dve.drain()
                dve.wait_ge(s_l, m + 1)
                V.tensor_tensor(dl[:, s, :], dl[:, s, :], lab, ALU.add).then_inc(s_dl, 1)
                dve.drain()
                dve.wait_ge(s_ldt[dt % 3], q * (16 * SLOT_TILES[dt % 3]) + 16 * (dt // 3 + 1))
                dve.wait_ge(s_bu, q * NT + max(2 * dt - 2, 0))
                V.tensor_tensor(dx[:, s, :], dl[:, s, :], xt[:, dt % 3, :], ALU.mult).then_inc(s_dx, 1)

            def scan(q, k):
                dt, h = k // 2, k % 2
                slot = k % 3
                dve.wait_ge(s_bu, q * NT + k + 1)
                for j in range(NH // 2):
                    dve.wait_ge(s_dA, q * (4 * NT) + 4 * k + j + 1)
                    for i in range(2):
                        n = 2 * j + i
                        last = V.tensor_tensor_scan(Tr[:, slot, n, :], pA[:, j % 2, i, :], Tr[:, slot, n, :],
                                                    hst[:, dt, h * NH + n:h * NH + n + 1], ALU.mult, ALU.add)
                    last.then_inc(s_dAf[j % 2], 1)
                dve.drain()
                V.tensor_copy(hst[:, dt, h * NH:(h + 1) * NH], Tr[:, slot, 0:NH, TC - 1]).then_inc(s_h, 1)
                if POOL_C < NH:
                    dve.drain()
                    if dt == 0:
                        dve.wait_ge(s_ldc[h], q * 32 + 32)
                    rest = Tr[:, slot, POOL_C:NH, :]
                    V.tensor_tensor(rest, rest, Cb[:, h * NH + POOL_C:(h + 1) * NH, :], ALU.mult)

            def reduce(q, k):
                dt, h = k // 2, k % 2
                s = dt % 3
                if POOL_C < NH:
                    dve.drain()
                dve.wait_ge(s_cm, q * NT + k + 1)
                if h == 0:
                    V.tensor_reduce(Tr[:, (k + 1) % 3, NH, :], Tr[:, k % 3, 0:NH, :].rearrange("p n t -> p t n"),
                                    AX.X, ALU.add).then_inc(s_rd, 1)
                else:
                    V.tensor_reduce(Tr[:, (k + 1) % 3, NH, :], Tr[:, k % 3, :, :].rearrange("p n t -> p t n"),
                                    AX.X, ALU.add)
                    dve.drain()
                    V.scalar_tensor_tensor(xt[:, s, :], xt[:, s, :], Dp[:, dt:dt + 1], Tr[:, (k + 1) % 3, NH, :],
                                           ALU.mult, ALU.add).then_inc(s_y, 1)
                    V.drain().then_inc(s_rd, 1)

            def opening(a):
                if a.kind == 2:
                    add_y(a, 0)
                unit_stats(a)
                unit_refine(a.u)
                low_part(a, 0)
                low_part(a, 1)

            def new_batch():
                dve.drain()
                V.memset(hst[:, :, :], 0.0)
                dve.drain()

            def closing(i, q, more_chunks, next_y):
                if more_chunks:
                    delta(i, 0)
                if q is not None:
                    dve.drain()
                    reduce(q, NT - 1)

            def unit(a, b):
                def half(h):
                    k = a.half_at(h)
                    if k is None:
                        return
                    scan(a.q, k)
                    if k % 2 == 0 and k // 2 + 1 < KD:
                        delta(a.q, k // 2 + 1)
                    if k > 0:
                        reduce(a.q, k - 1)

                if b and b.y_early:
                    add_y(b, 0)
                route(a)
                late_y = b and b.kind == 2 and not b.y_early
                if late_y:
                    add_y(b, 0)
                elif b:
                    unit_stats(b)
                half(0)
                if late_y:
                    unit_stats(b)
                if b:
                    unit_refine(b.u)
                half(1)
                half(2)
                if b:
                    low_part(b, 0)
                result(a, 0)
                half(3)
                if b:
                    low_part(b, 1)
                result(a, 1)
                if a.kind == 1:
                    dve.drain()
                    stats("ln2", xin[:, a.p, :], s_mv2)
                half(4)
                if a.kind == 1:
                    refine("ln2", 1.0, s_sd2, s_rs2, a.w)
                for h in range(5, 8):
                    half(h)

            schedule(dve, unit, opening, closing, new_batch)


def kernel(L0_attn_x, L0_attn_W_xproj, L0_attn_W_dt, L0_attn_b_dt, L0_attn_A_log, L0_attn_D_param,
           L0_ffn_A, L0_ffn_B, L0_ffn_W, L0_ffn_bias):
    import numpy as np
    import concourse.bacc as bacc
    from concourse.bass_utils import run_bass_kernel_spmd

    c = np.ascontiguousarray
    x = np.asarray(L0_attn_x)
    D = x.shape[2]
    A, B, W = np.asarray(L0_ffn_A), np.asarray(L0_ffn_B), np.asarray(L0_ffn_W)
    blocks = D // P
    arrays = {
        "x": c(x),
        "AT": c(A.reshape(-1, D).T),
        "BT": c(B.transpose(0, 2, 1).reshape(-1, B.shape[1])),
        "WT": c(W.T),
        "bias": c(np.asarray(L0_ffn_bias).reshape(1, -1)),
        "WxT": c(np.asarray(L0_attn_W_xproj).T),
        "WdtT": c(np.asarray(L0_attn_W_dt).T),
        "b_dt": c(np.asarray(L0_attn_b_dt).reshape(blocks, P).T),
        "A_log": c(np.asarray(L0_attn_A_log).reshape(blocks, P, -1).transpose(1, 0, 2)),
        "D_par": c(np.asarray(L0_attn_D_param).reshape(blocks, P).T),
    }
    nc = bacc.Bacc("TRN2", target_bir_lowering=False, num_devices=1)
    args = [nc.dram_tensor(n, a.shape, mybir.dt.from_np(a.dtype), kind="ExternalInput").ap() for n, a in arrays.items()]
    out = nc.dram_tensor("out", x.shape, mybir.dt.float32, kind="ExternalOutput").ap()
    build(nc, *args, out)
    r = run_bass_kernel_spmd(nc, [arrays], core_ids=[0])
    return r.results[0]["out"]
```
